# Optimizing a Trainium2 kernel written in Bass

```python
import numpy as np
import jax
import jax.numpy as jnp

def _softmax(x, axis=-1):
    return jax.nn.softmax(x, axis=axis)

def _gelu(x):
    return jax.nn.gelu(x, approximate=True)

def _silu(x):
    return jax.nn.silu(x)

def _sigmoid(x):
    return jax.nn.sigmoid(x)

def _layernorm(x, axis=-1, eps=1e-05):
    m = jnp.mean(x, axis=axis, keepdims=True)
    v = jnp.var(x, axis=axis, keepdims=True)
    return (x - m) / jnp.sqrt(v + eps)

def _scatter_add(tgt, idx, src, axis=0):
    return tgt.at[idx].add(src)

def _segment_sum(src, seg, n):
    return jax.ops.segment_sum(src, seg, n)
kernel_name = 'mk_adaln_ffn_d1_seqx_r4_30d875'

def setup_inputs(seed: int=0):
    np.random.seed(seed)
    _w = jnp.asarray

    def _rec_inputs():
        import jax
        import jax.numpy as jnp
        _rk = jax.random.key(seed)
        x = -0.000125 + 0.9999 * jax.random.normal(jax.random.fold_in(_rk, 1), (2, 1024, 256), jnp.float32)
        _lenS = 1024 - jax.random.randint(jax.random.fold_in(_rk, 7), (2,), 0, max(1, 1024 // 4) + 1, jnp.int32)
        _lenS2 = 1024 - jax.random.randint(jax.random.fold_in(_rk, 8), (2,), 0, max(1, 1024 // 4) + 1, jnp.int32)
        cond_1024 = 0.00513981 + 1.0024 * jax.random.normal(jax.random.fold_in(_rk, 11), (2, 256), jnp.float32)
        return (x, cond_1024)
    x, cond_1024 = _rec_inputs()

    def _L0_cond_setup():
        import jax, jax.numpy as jnp
        import numpy as np
        IN_FEATURES = 256
        OUT_FEATURES = 256
        BATCH = 32
        SEQ = 256
        EPS = 1e-08
        key = jax.random.key(seed)
        k1, k2, k3 = jax.random.split(key, 3)
        Efou = jax.random.normal(k1, (BATCH, SEQ, IN_FEATURES), dtype=jnp.float32)
        y = jax.random.normal(k2, (BATCH, IN_FEATURES), dtype=jnp.float32)
        weight = jax.random.normal(k3, (IN_FEATURES, OUT_FEATURES), dtype=jnp.float32)
        return {'Efou': Efou, 'y': y, 'weight': weight}
    _L0_cond_all = _L0_cond_setup()
    _L0_cond_in = {k: v for k, v in _L0_cond_all.items() if k in ('weight',)}
    del _L0_cond_all

    def _L0_ffn_setup():
        import jax, jax.numpy as jnp
        import numpy as np
        NUM_EXPERTS = 8
        NUM_LANGS = 4
        TOP_K = 2
        D_MODEL = 256
        EXPERT_SIZE = 1024
        B, S = (2, 512)
        key = jax.random.key(seed)
        ks = jax.random.split(key, 6)

        def xavier(k, shape, fan_in, fan_out):
            a = float(np.sqrt(6.0 / (fan_in + fan_out)))
            return jax.random.uniform(k, shape, jnp.float32, -a, a)
        return {'x': jax.random.normal(ks[0], (B, S, D_MODEL), jnp.float32), 'router_w': xavier(ks[1], (NUM_EXPERTS, D_MODEL), D_MODEL, NUM_EXPERTS), 'router_b': jnp.zeros((NUM_EXPERTS,), jnp.float32), 'lang_w': xavier(ks[2], (NUM_LANGS, D_MODEL), D_MODEL, NUM_LANGS), 'lang_b': jnp.zeros((NUM_LANGS,), jnp.float32), 'w1': xavier(ks[3], (NUM_EXPERTS, D_MODEL, EXPERT_SIZE), D_MODEL, EXPERT_SIZE), 'b1': jnp.zeros((NUM_EXPERTS, EXPERT_SIZE), jnp.float32), 'w2': xavier(ks[4], (NUM_EXPERTS, EXPERT_SIZE, D_MODEL), EXPERT_SIZE, D_MODEL), 'b2': jnp.zeros((NUM_EXPERTS, D_MODEL), jnp.float32)}
    _L0_ffn_all = _L0_ffn_setup()
    _L0_ffn_in = {k: v for k, v in _L0_ffn_all.items() if k in ('router_w', 'router_b', 'lang_w', 'lang_b', 'w1', 'b1', 'w2', 'b2')}
    del _L0_ffn_all
    return {'x': x, 'cond_1024': cond_1024, 'L0_cond_weight': _L0_cond_in['weight'], 'L0_ffn_router_w': _L0_ffn_in['router_w'], 'L0_ffn_router_b': _L0_ffn_in['router_b'], 'L0_ffn_lang_w': _L0_ffn_in['lang_w'], 'L0_ffn_lang_b': _L0_ffn_in['lang_b'], 'L0_ffn_w1': _L0_ffn_in['w1'], 'L0_ffn_b1': _L0_ffn_in['b1'], 'L0_ffn_w2': _L0_ffn_in['w2'], 'L0_ffn_b2': _L0_ffn_in['b2']}

def reference(x, cond_1024, L0_cond_weight, L0_ffn_router_w, L0_ffn_router_b, L0_ffn_lang_w, L0_ffn_lang_b, L0_ffn_w1, L0_ffn_b1, L0_ffn_w2, L0_ffn_b2):
    import jax
    import jax.numpy as jnp

    def _L0_cond_ref(Efou, y, weight):
        import jax, jax.numpy as jnp
        import numpy as np
        IN_FEATURES = 256
        OUT_FEATURES = 256
        BATCH = 32
        SEQ = 256
        EPS = 1e-08
        scale = 1.0 / np.sqrt(np.float32(weight.shape[0]))
        ys = y * scale
        d = jax.lax.rsqrt(jnp.einsum('bi,io->bo', ys * ys, weight * weight) + EPS)
        out = jnp.einsum('bsi,io->bso', Efou * ys[:, None, :], weight) * d[:, None, :]
        return out

    def _L0_ffn_ref(x, router_w, router_b, lang_w, lang_b, w1, b1, w2, b2):
        import jax, jax.numpy as jnp
        import numpy as np
        NUM_EXPERTS = 8
        NUM_LANGS = 4
        TOP_K = 2
        D_MODEL = 256
        EXPERT_SIZE = 1024
        B, S = (2, 512)
        lang_logits = x @ lang_w.T + lang_b
        lang_probs = jax.nn.softmax(lang_logits, axis=-1)
        lp_pad = jnp.pad(lang_probs, ((0, 0), (0, 0), (0, 1)))
        idx = jnp.arange(NUM_EXPERTS) % NUM_LANGS
        expert_weights = lp_pad[..., idx] + lp_pad[..., idx + 1]
        router_logits = x @ router_w.T + router_b + 0.1 * expert_weights
        router_probs = jax.nn.softmax(router_logits, axis=-1)
        top_p, top_i = jax.lax.top_k(router_probs, TOP_K)
        top_p = top_p / top_p.sum(axis=-1, keepdims=True)
        h = jax.nn.gelu(jnp.einsum('bsd,edh->bseh', x, w1) + b1, approximate=False)
        expert_out = jnp.einsum('bseh,ehd->bsed', h, w2) + b2
        sel = jnp.take_along_axis(expert_out, top_i[..., None], axis=2)
        return (top_p[..., None] * sel).sum(axis=2)
    x = x + _L0_ffn_ref(_L0_cond_ref(x, cond_1024, L0_cond_weight), L0_ffn_router_w, L0_ffn_router_b, L0_ffn_lang_w, L0_ffn_lang_b, L0_ffn_w1, L0_ffn_b1, L0_ffn_w2, L0_ffn_b2)
    return x

_drawn_inputs = setup_inputs


def setup_inputs(seed=0):
    import zlib

    import numpy as np

    out = dict(_drawn_inputs(seed))
    spreads = {'L0_ffn_router_b': (0.0, 0.1),
     'L0_ffn_lang_b': (0.0, 2.0),
     'L0_ffn_b1': (0.0, 0.1),
     'L0_ffn_b2': (0.0, 0.1)}
    factors = {}
    for name, (base, spread) in spreads.items():
        noise = np.random.default_rng([zlib.crc32(name.encode()), seed]).standard_normal(out[name].shape)
        drawn = base * np.exp(spread * noise) if base else spread * noise
        out[name] = jnp.asarray(drawn.astype(out[name].dtype))
    for name, factor in factors.items():
        out[name] = (out[name] * factor).astype(out[name].dtype)
    return out
```

```python
from contextlib import ExitStack

import concourse.bass as bass
from concourse import mybir

F32, F16, I32, U32 = mybir.dt.float32, mybir.dt.float16, mybir.dt.int32, mybir.dt.uint32
ALU, ACT, AX = mybir.AluOpType, mybir.ActivationFunctionType, mybir.AxisListType
RED = bass.bass_isa.ReduceOp

P = 128
NB, SEQ, D = 2, 1024, 256
E, L, F = 8, 4, 1024
NR = E + L
N = NB * SEQ
T = N // P
TB = T // NB
K = 2
NT = N * K // P + E - 1
KD, KF = D // P, F // P
GH = KF // 2
ROW = D + E
EPS = 1e-8
HALF = KD * F
SLOTS = 4
RING = 3
NH = 2 * RING
BIG = 1e30

FIELD_SCALE = 268 - 64
FIELD_GELU = 27
FIELD_H = 389 - 128
FIELD_HB = 267
FIELD_O = 113 + 64

C_GELU, C_H, C_O, C_P, NCUR = KF, KF + 1, KF + 2, KF + 3, KF + 4


def adaln_moe(nc, x, cond, cw, rw, rb, lw, lb, w1, b1, w2, b2, out):
    y_rows = nc.dram_tensor("y_rows", (N + P, ROW), F32, kind="Internal").ap()
    x_tiles = x.rearrange("b (t p) d -> p (b t) d", p=P)
    w1_v = w1.rearrange("e (k p) f -> e p k f", p=P)
    w2_v = w2.rearrange("e (c p) d -> e p c d", p=P)

    ctx = ExitStack()
    with ctx:
        def sb(name, shape, dt=F32):
            return ctx.enter_context(nc.sbuf_tensor(name, shape, dt))

        def sem(name):
            return ctx.enter_context(nc.semaphore(name))

        wsp = sb("wsp", [P, E, 4 * HALF], F16)
        stage = sb("stage", [P, SLOTS, HALF])
        pay = sb("pay", [P, T * ROW])
        onehot = sb("onehot", [P, K * T * P], F16)
        b2bc = sb("b2bc", [P, E, D])
        tilehot = sb("tilehot", [P, K * T, NT], F16)
        rows = sb("rows", [P, RING, ROW])
        scratch = wsp[:, E - 2, :].bitcast(F32)
        xin = wsp[:, E - 1, :].bitcast(F32).rearrange("p (t d) -> p t d", t=T)
        at = [0]

        def carve(n):
            at[0] += n
            assert at[0] <= 2 * HALF
            return scratch[:, at[0] - n:at[0]]

        W = carve(KD * D).rearrange("p (k d) -> p k d", k=KD)
        WT = carve(KD * D).rearrange("p (o i) -> p o i", o=KD)
        Wsq = carve(KD * D).rearrange("p (k d) -> p k d", k=KD)
        Wp = carve(NB * KD * (D + NR)).rearrange("p (b k n) -> p b k n", b=NB, k=KD)
        xT = carve(2 * D).rearrange("p (s n) -> p s n", s=2)
        ident = sb("ident", [P, P])
        tri = sb("tri", [P, P], F16)
        ones = sb("ones", [P, P], F16)
        iota = sb("iota", [P, P], I32)
        first = sb("first", [P, E], I32)
        home = sb("home", [P, E], I32)
        tok1 = sb("tok1", [P, T], I32)
        padi = sb("padi", [P, 1], I32)
        padf = sb("padf", [P, 1])
        tiles_i = sb("tiles_i", [1, NT - E, E], I32)
        te = sb("te", [1, NT], I32)
        condT = sb("condT", [P, KD, NB])
        ys = sb("ys", [P, KD, NB])
        ysq = sb("ysq", [P, KD, NB])
        RL = sb("RL", [NR, D])
        biasr = sb("biasr", [P, NR])
        R = sb("R", [P, KD, NR])
        Rd = sb("Rd", [P, NB, KD, NR])
        dv = sb("dv", [P, 5, KD * NB])
        dcol = sb("dcol", [P, KD, NB])
        b1r = sb("b1r", [E * KF, P])
        tab = sb("tab", [P, E, NCUR])
        cur = sb("cur", [P, RING, NCUR])
        wsum = sb("wsum", [P, 2 * E])
        wmax = sb("wmax", [P, 2 * E])
        wt = sb("wt", [P, 2 * E], I32)
        wfield = sb("wfield", [P, 2 * E], I32)
        wscale = sb("wscale", [P, 2 * E])
        ysum = sb("ysum", [P, T // 4])
        ysm = sb("ysm", [P, 1])
        ymax = sb("ymax", [P, 1])
        yt = sb("yt", [P, 1], I32)
        yfield = sb("yfield", [P, 1], I32)
        yscale = sb("yscale", [P, 1])
        bmx = sb("bmx", [P, E])
        bmax = sb("bmax", [P, E])
        bfield = sb("bfield", [P, E], I32)
        fld = sb("fld", [P, 4, E])
        fldi = sb("fldi", [P, 3, E], I32)
        s1 = sb("s1", [P, 8, T])
        M16 = sb("M16", [P, T, E], F16)
        Mt = sb("Mt", [P, E], F16)
        tl = sb("tl", [P, 6, E])
        tli = sb("tli", [P, 2, E], I32)
        cmp = sb("cmp", [1, NT - E, E])
        tef = sb("tef", [1, NT - E])
        slot = sb("slot", [P, K, T])
        sloti = sb("sloti", [P, 3, K * T], I32)
        idx = sb("idx", [P, NT], U32)
        padv = sb("padv", [P, NT])
        warm = sb("warm", [P, 1])

        route_at = [0]

        def share(*shape):
            n = 1
            for q in shape:
                n *= q
            route_at[0] += n
            assert route_at[0] <= E * D
            flat = b2bc[:, :, :].rearrange("p e d -> p (e d)")[:, route_at[0] - n:route_at[0]]
            return flat.rearrange("p (t e) -> p t e", t=shape[0]) if len(shape) == 2 else flat.rearrange(
                "p (k t e) -> p k t e", k=shape[0], t=shape[1])

        lg, lpp, le = share(T, NR), share(T, L + 1), share(T, L)
        eq, r2, oh = share(T, E), share(T, E), share(K, T, E)

        payv = pay[:, :].rearrange("p (t r) -> p t r", t=T)
        h32 = pay[:, 0:2 * GH * P].rearrange("p (g n) -> p g n", g=2)
        hsp = pay[:, 2 * GH * P:2 * GH * P + NH * GH * P].bitcast(F16).rearrange(
            "p (h s c n) -> p h s c n", h=NH, s=2, c=GH)
        ohv = onehot[:, :].rearrange("p (c s) -> p c s", s=P)
        xsp = onehot[:, 0:RING * 2 * D].rearrange("p (r s k n) -> p r s k n", r=RING, s=2, k=KD)
        outb = onehot[:, RING * 2 * D:RING * 4 * D].bitcast(F32).rearrange("p (r n) -> p r n", r=RING)

        ps = ctx.enter_context(nc.psum_tensor("ps", [P, 8, 512], F32))
        HB, OB, XB, MB = 0, 3, 6, 7

        consts = sem("consts"); small_in = sem("small_in"); x_in = [sem(f"x_in{c}") for c in range(4)]
        w_in = [sem(f"w_in{i}") for i in range(SLOTS)]
        b2_in = sem("b2_in"); pads_out = sem("pads_out"); x_copied = sem("x_copied"); y_written = sem("y_written")
        zero_ready = sem("zero_ready")
        wt_psum = sem("wt_psum"); wt_ready = sem("wt_ready"); rb_psum = sem("rb_psum")
        sq_ready = sem("sq_ready"); v_psum = sem("v_psum"); v_ready = sem("v_ready"); v_root = sem("v_root")
        d_ready = sem("d_ready"); rd_ready = sem("rd_ready"); d_psum = sem("d_psum"); wr_psum = sem("wr_psum")
        wp_ready = sem("wp_ready"); b1_ready = sem("b1_ready"); b1_max = sem("b1_max")
        xt_psum = sem("xt_psum"); xt_ready = sem("xt_ready"); y_psum = sem("y_psum"); y_ready = sem("y_ready")
        y_sq = sem("y_sq"); ym_ready = sem("ym_ready"); y_max = sem("y_max")
        lang_in = sem("lang_in"); lang_exp = sem("lang_exp"); gap_in = sem("gap_in"); gap_exp = sem("gap_exp")
        picked = sem("picked"); p_ready = sem("p_ready"); ranked = sem("ranked"); hot_ready = sem("hot_ready")
        mapped = sem("mapped"); idx_ready = sem("idx_ready"); te_ready = sem("te_ready")
        w_sq = sem("w_sq"); w_max = sem("w_max"); w_scaled = sem("w_scaled"); w_hi = sem("w_hi"); w_split = sem("w_split")
        tab_ready = sem("tab_ready")
        dve_step = sem("dve_step")
        gathered = [sem(f"gathered{r}") for r in range(RING)]
        t_done = sem("t_done"); x_hi = sem("x_hi"); x_split = sem("x_split")
        l1_done = sem("l1_done"); gelu_done = sem("gelu_done"); h_hi = sem("h_hi"); h_split = sem("h_split")
        l2_done = sem("l2_done"); o_read = sem("o_read"); o_ready = sem("o_ready"); added = sem("added")

        def expert_of(eng, j):
            return eng.value_load(te[0:1, bass.ds(j, 1)], min_val=0, max_val=E - 1)

        block = ctx.enter_context(nc.Block())

        @block.sync
        def _(sp):
            sp.dma_start(W, cw.rearrange("(k p) d -> p k d", p=P)).then_inc(small_in, 16)
            for b in range(NB):
                for k in range(KD):
                    sp.dma_start(condT[:, k, b:b + 1],
                                 cond[b, k * P:(k + 1) * P].rearrange("(p a) -> p a", a=1)).then_inc(small_in, 16)
            sp.dma_start(RL[0:E, :], rw).then_inc(small_in, 16)
            sp.dma_start(RL[E:NR, :], lw).then_inc(small_in, 16)
            sp.dma_start(biasr[:, 0:E], rb.rearrange("(a n) -> a n", a=1).broadcast_to([P, E])).then_inc(small_in, 16)
            sp.dma_start(biasr[:, E:NR], lb.rearrange("(a n) -> a n", a=1).broadcast_to([P, L])).then_inc(small_in, 16)
            sp.dma_start(b1r[:, :], b1.rearrange("e (c p) -> (e c) p", p=P)).then_inc(small_in, 16)
            for c in range(4):
                sp.dma_start(xin[:, 4 * c:4 * c + 4, :], x_tiles[:, 4 * c:4 * c + 4, :]).then_inc(x_in[c], 16)
            for n in range(2 * E):
                if n >= SLOTS:
                    sp.wait_ge(w_split, n - SLOTS + 1)
                src = (w1_v if n % 2 == 0 else w2_v)[n // 2]
                dst = stage[:, n % SLOTS, :].rearrange("p (k f) -> p k f", k=KD if n % 2 == 0 else KF)
                sp.dma_start(dst, src).then_inc(w_in[n % SLOTS], 16)
                if n == 3:
                    sp.wait_ge(zero_ready, 1)
                    sp.dma_start(y_rows[N:N + P, :], rows[:, 0, :]).then_inc(pads_out, 16)
                    sp.dma_start(out[N:N + P, :], rows[:, 0, 0:D]).then_inc(pads_out, 16)
                    sp.dma_start(out[0:N, :], x.rearrange("b s d -> (b s) d")).then_inc(x_copied, 16)
                if n == 9:
                    sp.wait_ge(p_ready, 1)
                    sp.dma_start(y_rows[0:N, :].rearrange("(t p) r -> p t r", p=P), payv).then_inc(y_written, 16)
                    sp.wait_ge(idx_ready, 1)
                    sp.dma_start(b2bc[:, :, :].rearrange("p e d -> p (e d)"),
                                 b2.rearrange("(a e) d -> a (e d)", a=1).broadcast_to([P, E * D])).then_inc(b2_in, 16)

        @block.gpsimd
        def _(pool):
            g = nc.gpsimd
            g.memset(ident[:, :], 0.0).then_inc(consts, 1)
            g.memset(tri[:, :], 1.0).then_inc(consts, 1)
            g.memset(ones[:, :], 1.0).then_inc(consts, 1)
            g.iota(iota[:, :], pattern=[[1, P]], base=0, channel_multiplier=0).then_inc(consts, 1)
            g.iota(first[:, :], pattern=[[-1, E]], base=E, channel_multiplier=0).then_inc(consts, 1)
            g.iota(home[:, :], pattern=[[P, E]], base=0, channel_multiplier=0).then_inc(consts, 1)
            g.iota(tok1[:, :], pattern=[[P, T]], base=1, channel_multiplier=1).then_inc(consts, 1)
            g.iota(padi[:, :], pattern=[[0, 1]], base=N + 1, channel_multiplier=1).then_inc(consts, 1)
            g.iota(tiles_i[:, :, :], pattern=[[1, NT - E], [0, E]], base=0, channel_multiplier=0).then_inc(consts, 1)
            g.iota(te[:, 0:E], pattern=[[1, E]], base=0, channel_multiplier=0).then_inc(consts, 1)
            g.memset(lpp[:, :, L:L + 1], 0.0).then_inc(consts, 1)
            g.memset(rows[:, 0, :], 0.0).then_inc(zero_ready, 1)
            pool.wait_ge(consts, 11)
            g.affine_select(out=ident[:, :], in_=ident[:, :], compare_op=ALU.not_equal, fill=1.0, base=0,
                            pattern=[[-1, P]], channel_multiplier=1).then_inc(consts, 1)
            g.affine_select(out=tri[:, :], in_=tri[:, :], compare_op=ALU.is_gt, fill=0.0, base=0,
                            pattern=[[1, P]], channel_multiplier=-1).then_inc(consts, 1)
            g.tensor_copy(padf[:, :], padi[:, :]).then_inc(consts, 1)

            def split_hi(n):
                e, o = n // 2, (n % 2) * 2 * HALF
                pool.wait_ge(w_sq, n + 1)
                g.partition_all_reduce(wmax[:, n:n + 1], wsum[:, n:n + 1], P, RED.max).then_inc(w_max, 1)
                if e == E - 2 and n % 2 == 0:
                    pool.wait_ge(y_psum, T)
                pool.wait_ge(w_scaled, n + 1)
                g.tensor_scalar(wsp[:, e, o:o + HALF], stage[:, n % SLOTS, :], wscale[:, n:n + 1], 1.0,
                                ALU.mult, ALU.mult).then_inc(w_hi, 1)

            pool.wait_ge(b1_ready, 1)
            g.partition_all_reduce(bmax[:, :], bmx[:, :], P, RED.max).then_inc(b1_max, 1)
            for n in range(6):
                split_hi(n)
            pool.wait_ge(ym_ready, 1)
            g.partition_all_reduce(ymax[:, :], ysm[:, :], P, RED.max).then_inc(y_max, 1)
            for n in range(6, 2 * E):
                split_hi(n)

            def gather(j):
                g.indirect_dma_start(out=rows[:, j % RING, :], out_offset=None, in_=y_rows,
                                     in_offset=bass.IndirectOffsetOnAxis(ap=idx[:, j:j + 1], axis=0)
                                     ).then_inc(gathered[j % RING], 16)

            pool.wait_ge(y_written, 16)
            pool.wait_ge(pads_out, 32)
            pool.wait_ge(idx_ready, 1)
            for j in range(RING):
                gather(j)
            pool.wait_ge(x_copied, 16)
            for j in range(NT):
                if j + RING < NT:
                    pool.wait_ge(x_split, j + 1)
                    gather(j + RING)
                pool.wait_ge(o_ready, j + 1)
                if j:
                    pool.wait_ge(added, 16 * j)
                g.indirect_dma_start(out=out, out_offset=bass.IndirectOffsetOnAxis(ap=idx[:, j:j + 1], axis=0),
                                     in_=outb[:, j % RING, :], in_offset=None,
                                     compute_op=ALU.add).then_inc(added, 16)
            pool.wait_ge(added, 16 * NT)

        @block.tensor
        def _(pe):
            mm, tr = nc.tensor.matmul, nc.tensor.transpose
            pe.wait_ge(consts, 14)
            pe.wait_ge(small_in, 16 * 10)
            for o in range(KD):
                for k in range(KD):
                    last = tr(ps[:, 0, (o * KD + k) * P:(o * KD + k + 1) * P], W[:, k, o * P:(o + 1) * P], ident[:, :])
            last.then_inc(wt_psum, 1)
            for k in range(KD):
                tr(ps[:, 1, k * NR:(k + 1) * NR], RL[:, k * P:(k + 1) * P], ident[0:NR, 0:NR])
            tr(ps[:, 1, 64:64 + E * KF], b1r[:, :], ident[0:E * KF, 0:E * KF]).then_inc(rb_psum, 1)
            pe.wait_ge(sq_ready, 1)
            for o in range(KD):
                for k in range(KD):
                    last = mm(ps[:, 2, o * NB:(o + 1) * NB], Wsq[:, k, o * P:(o + 1) * P], ysq[:, k, :],
                              start=(k == 0), stop=(k == KD - 1))
            last.then_inc(v_psum, 1)
            pe.wait_ge(d_ready, 1)
            for b in range(NB):
                for o in range(KD):
                    last = mm(ps[:, 3, b * D + o * P:b * D + (o + 1) * P],
                              dcol[:, o, b:b + 1].broadcast_to([P, P]), ident[:, :], start=True, stop=True)
            last.then_inc(d_psum, 1)
            pe.wait_ge(rd_ready, 1)
            pe.wait_ge(wt_ready, 1)
            for b in range(NB):
                for k in range(KD):
                    for o in range(KD):
                        last = mm(ps[:, 4, (b * KD + k) * NR:(b * KD + k + 1) * NR], WT[:, o, k * P:(k + 1) * P],
                                  Rd[:, b, o, :], start=(o == 0), stop=(o == KD - 1))
            last.then_inc(wr_psum, 1)

            def transpose_x(t):
                if t % 4 == 0:
                    pe.wait_ge(x_in[t // 4], 16)
                if t >= 2:
                    pe.wait_ge(xt_ready, t - 1)
                for k in range(KD):
                    last = tr(ps[:, 5 + t % 2, k * P:(k + 1) * P], xin[:, t, k * P:(k + 1) * P], ident[:, :])
                last.then_inc(xt_psum, 1)

            transpose_x(0)
            pe.wait_ge(wp_ready, 1)
            for t in range(T):
                if t + 1 < T:
                    transpose_x(t + 1)
                pe.wait_ge(xt_ready, t + 1)
                if t >= 2:
                    pe.wait_ge(y_ready, t - 1)
                for k in range(KD):
                    last = mm(ps[:, t % 2, 0:D + NR], xT[:, t % 2, k * P:(k + 1) * P], Wp[:, t // TB, k, :],
                              start=(k == 0), stop=(k == KD - 1))
                last.then_inc(y_psum, 1)

            pe.wait_ge(picked, 1)
            mm(ps[:, 2, 0:T * E], tri[:, :], M16[:, :, :].rearrange("p t e -> p (t e)"), start=True, stop=False)
            for t in range(T - 1):
                mm(ps[:, 2, (t + 1) * E:T * E].rearrange("p (a e) -> p a e", e=E), ones[:, :],
                   M16[:, t:t + 1, :].broadcast_to([P, T - 1 - t, E]), start=False, stop=(t == T - 2))
            mm(ps[:, 3, 0:E], ones[:, :], Mt[:, :], start=True, stop=True).then_inc(ranked, 1)
            for c in range(K * T):
                if c % T == 0:
                    pe.wait_ge(hot_ready, c // T + 1)
                last = mm(ps[:, MB, 0:NT], ohv[:, c, :], tilehot[:, c, :], start=(c == 0), stop=(c == K * T - 1))
            last.then_inc(mapped, 1)

            def transpose_rows(j, i, u):
                pe.wait_ge(gathered[u % RING], 16 * (i + 1 + u // RING))
                if not (isinstance(j, int) and j == 0):
                    pe.wait_ge(x_split, j)
                for k in range(KD):
                    last = tr(ps[:, XB, k * P:(k + 1) * P], rows[:, u % RING, k * P:(k + 1) * P], ident[:, :])
                last.then_inc(t_done, 1)

            def up(j, u):
                e = expert_of(pe, j)
                pe.wait_ge(w_split, 2 * e + 1)
                pe.wait_ge(x_split, j + 1)
                for gg in range(2):
                    n = 2 * u + gg
                    if not (isinstance(j, int) and 2 * j + gg < RING):
                        pe.wait_ge(gelu_done, 2 * j + gg - 2)
                    for c in range(GH):
                        cc = gg * GH + c
                        steps = [(w, s, k) for w, s in ((0, 0), (0, 1), (1, 0)) for k in range(KD)]
                        for q, (w, s, k) in enumerate(steps):
                            o = w * HALF + k * F + cc * P
                            last = mm(ps[:, HB + n % RING, c * P:(c + 1) * P],
                                      wsp[:, bass.ds(e, 1), o:o + P].rearrange("p a f -> p (a f)"),
                                      xsp[:, u % RING, s, k, :], start=(q == 0), stop=(q == len(steps) - 1))
                    last.then_inc(l1_done, 1)

            def down(j, u):
                e = expert_of(pe, j)
                pe.wait_ge(w_split, 2 * e + 2)
                if not (isinstance(j, int) and j < RING):
                    pe.wait_ge(o_read, j - RING + 1)
                for c in range(KF):
                    if c % GH == 0:
                        pe.wait_ge(h_split, 2 * j + c // GH + 1)
                    for s, w in ((0, 0), (0, 1), (1, 0)):
                        o = (2 + w) * HALF + c * D
                        last = mm(ps[:, OB + u % RING, 0:D], hsp[:, (2 * u + c // GH) % NH, s, c % GH, :],
                                  wsp[:, bass.ds(e, 1), o:o + D].rearrange("p a f -> p (a f)"),
                                  start=(c == 0 and s == 0 and w == 0), stop=(c == KF - 1 and s == 1))
                last.then_inc(l2_done, 1)

            pe.wait_ge(te_ready, 1)
            transpose_rows(0, 0, 0)
            transpose_rows(1, 0, 1)
            up(0, 0)
            for u in range(RING):
                transpose_rows(u + 2, 0, u + 2)
                up(u + 1, u + 1)
                down(u, u)
            with pe.Fori(1, NT // RING - 1) as i:
                for u in range(RING):
                    transpose_rows(RING * i + u + 2, i, u + 2)
                    up(RING * i + u + 1, u + 1)
                    down(RING * i + u, u)
            i = NT // RING - 1
            transpose_rows(NT - 1, i, 2)
            up(NT - 2, 1)
            down(NT - 3, 0)
            up(NT - 1, 2)
            down(NT - 2, 1)
            down(NT - 1, 2)

        @block.scalar
        def _(act):
            a = nc.scalar
            act.wait_ge(wt_psum, 1)
            a.activation(WT.rearrange("p o i -> p (o i)"), ps[:, 0, :], ACT.Copy).then_inc(wt_ready, 1)
            act.wait_ge(v_ready, 1)
            a.activation(dv[:, 1, :], dv[:, 0, :], ACT.Sqrt).then_inc(v_root, 1)

            def square_weights(n):
                e, o = n // 2, (n % 2) * 2 * HALF + HALF
                act.wait_ge(w_in[n % SLOTS], 16 * (n // SLOTS + 1))
                if e >= E - 2:
                    act.wait_ge(y_psum, T)
                a.activation(wsp[:, e, o:o + HALF], stage[:, n % SLOTS, :], ACT.Square,
                             accum_out=wsum[:, n:n + 1]).then_inc(w_sq, 1)

            for t in range(T):
                act.wait_ge(xt_psum, t + 1)
                if t >= 2:
                    act.wait_ge(y_psum, t - 1)
                a.activation(xT[:, t % 2, :], ps[:, 5 + t % 2, 0:D], ACT.Copy).then_inc(xt_ready, 1)
                if t % 4 == 3:
                    c = t // 4
                    act.wait_ge(y_ready, t + 1)
                    a.activation(ohv[:, 8 * c:8 * c + 8, :].rearrange("p (t b) s -> p t (b s)", b=2),
                                 payv[:, 4 * c:4 * c + 4, 0:D], ACT.Square,
                                 accum_out=ysum[:, c:c + 1]).then_inc(y_sq, 1)
                if t in (2, 4, 6, 8, 10, 12):
                    square_weights(t // 2 - 1)
            act.wait_ge(lang_in, 1)
            a.activation(le[:, :, :], lpp[:, :, 0:L], ACT.Exp).then_inc(lang_exp, 1)
            for n in (6, 7):
                square_weights(n)
            act.wait_ge(gap_in, 1)
            a.activation(s1[:, 5, :], s1[:, 4, :], ACT.Exp).then_inc(gap_exp, 1)
            for n in range(8, 2 * E):
                square_weights(n)
            a.activation(warm[:, :], s1[:, 4, 0:1], ACT.Gelu)

            def gelus(j, u):
                act.wait_ge(x_split, j + 1)
                for gg in range(2):
                    n = 2 * u + gg
                    act.wait_ge(l1_done, 2 * j + gg + 1)
                    if not (isinstance(j, int) and j == 0):
                        act.wait_ge(h_split, 2 * j + gg - 1)
                    for c in range(GH):
                        cc = gg * GH + c
                        last = a.activation(h32[:, gg, c * P:(c + 1) * P], ps[:, HB + n % RING, c * P:(c + 1) * P],
                                            ACT.Gelu, bias=cur[:, u, cc:cc + 1], scale=cur[:, u, C_GELU:C_GELU + 1])
                    last.then_inc(gelu_done, 1)

            for u in range(RING):
                gelus(u, u)
            with act.Fori(1, NT // RING) as i:
                for u in range(RING):
                    gelus(RING * i + u, u)

        @block.vector
        def _(dve):
            v = nc.vector
            steps = [0]

            def step(ins):
                steps[0] += 1
                ins.then_inc(dve_step, 1)
                dve.wait_ge(dve_step, steps[0])

            dve.wait_ge(small_in, 16 * 10)
            step(v.tensor_scalar(ys[:, :, :], condT[:, :, :], D ** -0.5, None, ALU.mult))
            step(v.tensor_tensor(ysq[:, :, :], ys[:, :, :], ys[:, :, :], ALU.mult))
            v.tensor_tensor(Wsq, W, W, ALU.mult).then_inc(sq_ready, 1)
            dve.wait_ge(rb_psum, 1)
            step(v.tensor_copy(R[:, :, :], ps[:, 1, 0:KD * NR].rearrange("p (k n) -> p k n", k=KD)))
            step(v.tensor_copy(tab[:, :, 0:KF], ps[:, 1, 64:64 + E * KF].rearrange("p (e c) -> p e c", e=E)))
            v.tensor_reduce(bmx[:, :], tab[:, :, 0:KF], AX.X, ALU.max, apply_absolute_value=True).then_inc(b1_ready, 1)
            dve.wait_ge(v_psum, 1)
            v.tensor_scalar(dv[:, 0, :], ps[:, 2, 0:KD * NB], EPS, None, ALU.add).then_inc(v_ready, 1)
            dve.wait_ge(v_root, 1)
            step(v.reciprocal(dv[:, 2, :], dv[:, 1, :]))
            step(v.tensor_tensor(dv[:, 3, :], dv[:, 2, :], dv[:, 2, :], ALU.mult))
            step(v.tensor_tensor(dv[:, 4, :], dv[:, 3, :], dv[:, 0, :], ALU.mult))
            step(v.tensor_scalar(dv[:, 3, :], dv[:, 4, :], -0.5, 1.5, ALU.mult, ALU.add))
            dve.wait_ge(v_ready, 1)
            v.tensor_tensor(dcol[:, :, :].rearrange("p o b -> p (o b)"), dv[:, 2, :], dv[:, 3, :],
                            ALU.mult).then_inc(d_ready, 1)
            dve.wait_ge(d_ready, 1)
            for b in range(NB):
                last = v.tensor_tensor(Rd[:, b, :, :], R[:, :, :], dcol[:, :, b:b + 1].broadcast_to([P, KD, NR]), ALU.mult)
            last.then_inc(rd_ready, 1)
            dve.wait_ge(d_psum, 1)
            for b in range(NB):
                for k in range(KD):
                    v.scalar_tensor_tensor(out=Wp[:, b, k, 0:D], in0=W[:, k, :], scalar=ys[:, k, b:b + 1],
                                           in1=ps[:, 3, b * D:(b + 1) * D], op0=ALU.mult, op1=ALU.mult)
            dve.wait_ge(wr_psum, 1)
            for b in range(NB):
                last = v.tensor_tensor(
                    Wp[:, b, :, D:D + NR],
                    ps[:, 4, b * KD * NR:(b + 1) * KD * NR].rearrange("p (k n) -> p k n", k=KD),
                    ys[:, :, b:b + 1].broadcast_to([P, KD, NR]), ALU.mult)
            last.then_inc(wp_ready, 1)
            dve.wait_ge(b1_max, 1)
            step(v.tensor_scalar(bfield[:, :], bmax[:, :].bitcast(I32), 23, None, ALU.logical_shift_right))
            step(v.tensor_scalar(fld[:, 3, :], bfield[:, :], -1.0, float(FIELD_HB), ALU.mult, ALU.add))

            def scale_weights(n):
                dve.wait_ge(w_max, n + 1)
                step(v.tensor_scalar(wt[:, n:n + 1], wmax[:, n:n + 1].bitcast(I32), 24, None, ALU.logical_shift_right))
                step(v.tensor_scalar(wfield[:, n:n + 1], wt[:, n:n + 1], -1.0, float(FIELD_SCALE), ALU.mult, ALU.add))
                v.tensor_scalar(wscale[:, n:n + 1].bitcast(I32), wfield[:, n:n + 1], 23, None,
                                ALU.logical_shift_left).then_inc(w_scaled, 1)

            def split_lo(n):
                e, o = n // 2, (n % 2) * 2 * HALF
                dve.wait_ge(w_hi, n + 1)
                v.scalar_tensor_tensor(out=wsp[:, e, o + HALF:o + 2 * HALF], in0=stage[:, n % SLOTS, :],
                                       scalar=wscale[:, n:n + 1], in1=wsp[:, e, o:o + HALF],
                                       op0=ALU.mult, op1=ALU.subtract).then_inc(w_split, 1)

            for t in range(T):
                dve.wait_ge(y_psum, t + 1)
                v.tensor_tensor(lg[:, t, :], ps[:, t % 2, D:D + NR], biasr[:, :], ALU.add)
                v.tensor_copy(payv[:, t, 0:D], ps[:, t % 2, 0:D]).then_inc(y_ready, 1)
                if t in (4, 6, 8, 10, 12, 14):
                    scale_weights(t // 2 - 2)
                if t in (5, 7, 9, 11, 13, 15):
                    split_lo((t - 1) // 2 - 2)

            lang, route = lg[:, :, E:NR], lg[:, :, 0:E]

            def over(ap, n):
                return ap.rearrange("p (t a) -> p t a", a=1).broadcast_to([P, T, n])

            dve.wait_ge(y_ready, T)
            step(v.tensor_reduce(s1[:, 0, :], lang, AX.X, ALU.max))
            v.tensor_tensor(lpp[:, :, 0:L], lang, over(s1[:, 0, :], L), ALU.subtract).then_inc(lang_in, 1)
            dve.wait_ge(y_sq, 4)
            v.tensor_reduce(ysm[:, :], ysum[:, :], AX.X, ALU.max).then_inc(ym_ready, 1)
            dve.wait_ge(lang_exp, 1)
            step(v.tensor_reduce(s1[:, 1, :], le[:, :, :], AX.X, ALU.add))
            step(v.reciprocal(s1[:, 2, :], s1[:, 1, :]))
            step(v.tensor_tensor(lpp[:, :, 0:L], le[:, :, :], over(s1[:, 2, :], L), ALU.mult))
            step(v.tensor_tensor(le[:, :, :], lpp[:, :, 0:L], lpp[:, :, 1:L + 1], ALU.add))
            for q in range(E // L):
                last = v.scalar_tensor_tensor(out=route[:, :, q * L:(q + 1) * L], in0=le[:, :, :], scalar=0.1,
                                              in1=route[:, :, q * L:(q + 1) * L], op0=ALU.mult, op1=ALU.add)
            step(last)

            def pick(k, logits, m):
                step(v.tensor_reduce(s1[:, m, :], logits, AX.X, ALU.max))
                step(v.tensor_tensor(eq[:, :, :], logits, over(s1[:, m, :], E), ALU.is_equal))
                step(v.tensor_tensor(eq[:, :, :], eq[:, :, :],
                                     first[:, :].rearrange("p (a e) -> p a e", a=1).broadcast_to([P, T, E]), ALU.mult))
                step(v.tensor_reduce(s1[:, 3, :], eq[:, :, :], AX.X, ALU.max))
                step(v.tensor_tensor(oh[:, k, :, :], eq[:, :, :], over(s1[:, 3, :], E), ALU.is_equal))

            pick(0, route, 6)
            step(v.scalar_tensor_tensor(out=r2[:, :, :], in0=oh[:, 0, :, :], scalar=-BIG, in1=route,
                                        op0=ALU.mult, op1=ALU.add))
            pick(1, r2[:, :, :], 7)
            step(v.tensor_tensor(M16[:, :, :], oh[:, 0, :, :], oh[:, 1, :, :], ALU.add))
            with nc.allow_low_precision(reason="counts of at most 16"):
                v.tensor_reduce(Mt[:, :], M16[:, :, :].rearrange("p t e -> p e t"), AX.X, ALU.add).then_inc(picked, 1)
            v.tensor_tensor(s1[:, 4, :], s1[:, 7, :], s1[:, 6, :], ALU.subtract).then_inc(gap_in, 1)
            dve.wait_ge(gap_exp, 1)
            step(v.tensor_scalar(s1[:, 0, :], s1[:, 5, :], 1.0, None, ALU.add))
            step(v.reciprocal(s1[:, 1, :], s1[:, 0, :]))
            step(v.tensor_tensor(s1[:, 2, :], s1[:, 5, :], s1[:, 1, :], ALU.mult))
            step(v.tensor_tensor(eq[:, :, :], oh[:, 0, :, :], over(s1[:, 1, :], E), ALU.mult))
            step(v.tensor_tensor(r2[:, :, :], oh[:, 1, :, :], over(s1[:, 2, :], E), ALU.mult))
            v.tensor_tensor(payv[:, :, D:ROW], eq[:, :, :], r2[:, :, :], ALU.add).then_inc(p_ready, 1)

            dve.wait_ge(ranked, 1)
            step(v.tensor_scalar(tli[:, 0, :], ps[:, 3, 0:E], float(P - 1), None, ALU.add))
            step(v.tensor_scalar(tli[:, 1, :], tli[:, 0, :], 7, None, ALU.logical_shift_right))
            step(v.tensor_scalar(tl[:, 0, :], tli[:, 1, :], -1.0, 0.0, ALU.add, ALU.max))
            src = 0
            for d in (1, 2, 4):
                step(v.tensor_copy(tl[:, src + 1, 0:d], tl[:, src, 0:d]))
                step(v.tensor_tensor(tl[:, src + 1, d:E], tl[:, src, d:E], tl[:, src, 0:E - d], ALU.add))
                src += 1
            step(v.tensor_tensor(cmp[:, :, :], tiles_i[:, :, :],
                                 tl[0:1, src:src + 1, :].broadcast_to([1, NT - E, E]), ALU.is_ge))
            step(v.tensor_reduce(tef[:, :], cmp[:, :, :], AX.X, ALU.add))
            v.tensor_scalar(te[:, E:NT], tef[:, :], float(E - 1), None, ALU.min).then_inc(te_ready, 1)
            step(v.tensor_tensor(tl[:, 4, :], tl[:, src, :], tl[:, 0, :], ALU.subtract))
            step(v.tensor_scalar(tl[:, 5, :], tl[:, 4, :], float(P), float((E - 1) * P), ALU.mult, ALU.add))
            step(v.tensor_tensor(tl[:, 1, :], tl[:, 5, :], home[:, :], ALU.subtract))
            rank = ps[:, 2, 0:T * E].rearrange("p (t e) -> p t e", e=E)

            def each(ap):
                return ap.rearrange("p (a e) -> p a e", a=1).broadcast_to([P, T, E])

            dve.wait_ge(p_ready, 1)
            step(v.scalar_tensor_tensor(out=eq[:, :, :], in0=rank, scalar=float(P), in1=each(tl[:, 1, :]),
                                        op0=ALU.is_ge, op1=ALU.mult))
            step(v.tensor_tensor(r2[:, :, :], rank, eq[:, :, :], ALU.add))
            step(v.tensor_tensor(eq[:, :, :], r2[:, :, :], each(home[:, :]), ALU.add))
            for k in range(K):
                step(v.tensor_tensor(r2[:, :, :], oh[:, k, :, :], eq[:, :, :], ALU.mult))
                step(v.tensor_reduce(slot[:, k, :], r2[:, :, :], AX.X, ALU.add))
            step(v.tensor_copy(sloti[:, 0, :], slot[:, :, :].rearrange("p k t -> p (k t)")))
            v.tensor_scalar(sloti[:, 1, :], sloti[:, 0, :], 7, None, ALU.logical_shift_right)
            step(v.tensor_scalar(sloti[:, 2, :], sloti[:, 0, :], P - 1, None, ALU.bitwise_and))
            dve.wait_ge(y_max, 1)
            for k in range(K):
                def wide(ap, n):
                    return ap.rearrange("p (t a) -> p t a", a=1).broadcast_to([P, T, n])
                c = slice(k * T, (k + 1) * T)
                step(v.tensor_tensor(tilehot[:, c, :],
                                     iota[:, 0:NT].rearrange("p (a n) -> p a n", a=1).broadcast_to([P, T, NT]),
                                     wide(sloti[:, 1, c], NT), ALU.is_equal))
                v.tensor_tensor(tilehot[:, c, :], tilehot[:, c, :], wide(tok1[:, :], NT), ALU.mult)
                v.tensor_tensor(ohv[:, c, :], iota[:, :].rearrange("p (a n) -> p a n", a=1).broadcast_to([P, T, P]),
                                wide(sloti[:, 2, c], P), ALU.is_equal).then_inc(hot_ready, 1)
            dve.wait_ge(mapped, 1)
            step(v.tensor_scalar(padv[:, :], ps[:, MB, 0:NT], 0.0, padf[:, 0:1], ALU.is_equal, ALU.mult))
            v.scalar_tensor_tensor(out=idx[:, :], in0=ps[:, MB, 0:NT], scalar=-1.0, in1=padv[:, :],
                                   op0=ALU.add, op1=ALU.add).then_inc(idx_ready, 1)
            for n in range(6, 2 * E):
                scale_weights(n)
                split_lo(n)
            step(v.tensor_scalar(yt[:, :], ymax[:, :].bitcast(I32), 24, None, ALU.logical_shift_right))
            step(v.tensor_scalar(yfield[:, :], yt[:, :], -1.0, float(FIELD_SCALE), ALU.mult, ALU.add))
            step(v.tensor_scalar(yscale[:, :].bitcast(I32), yfield[:, :], 23, None, ALU.logical_shift_left))
            wt2 = wt[:, :].rearrange("p (e w) -> p e w", w=2)
            ytb = yt[:, :].broadcast_to([P, E])
            step(v.tensor_tensor(fld[:, 0, :], wt2[:, :, 0], ytb, ALU.add))
            step(v.tensor_scalar(fld[:, 1, :], fld[:, 0, :], -1.0, float(FIELD_H), ALU.mult, ALU.add))
            step(v.tensor_tensor(fld[:, 1, :], fld[:, 1, :], fld[:, 3, :], ALU.min))
            step(v.tensor_scalar(fld[:, 1, :], fld[:, 1, :], 1.0, 254.0, ALU.max, ALU.min))
            step(v.tensor_tensor(fld[:, 2, :], wt2[:, :, 1], fld[:, 1, :], ALU.subtract))
            step(v.tensor_scalar(fld[:, 2, :], fld[:, 2, :], float(FIELD_O), None, ALU.add))
            step(v.tensor_scalar(fld[:, 0, :], fld[:, 0, :], -float(FIELD_GELU), None, ALU.add))
            step(v.tensor_scalar(fldi[:, :, :], fld[:, 0:3, :], 1.0, 254.0, ALU.max, ALU.min))
            for q, c in ((0, C_GELU), (1, C_H), (2, C_O)):
                last = v.tensor_scalar(tab[:, :, c].bitcast(I32), fldi[:, q, :], 23, None, ALU.logical_shift_left)
            step(last)

            def split_x(j, u):
                e = expert_of(dve, j)
                r = u % RING
                dve.wait_ge(t_done, j + 1)
                if not (isinstance(j, int) and j < RING):
                    dve.wait_ge(o_ready, j - RING + 1)
                v.tensor_copy(cur[:, r, 0:C_P], tab[:, bass.ds(e, 1), 0:C_P].rearrange("p a c -> p (a c)"))
                v.tensor_copy(cur[:, r, C_P:NCUR], rows[:, r, bass.ds(e + D, 1)])
                v.tensor_scalar(xsp[:, r, 0, :, :].rearrange("p k n -> p (k n)"), ps[:, XB, 0:D], yscale[:, 0:1], None,
                                ALU.mult).then_inc(x_hi, 1)
                dve.wait_ge(x_hi, j + 1)
                v.scalar_tensor_tensor(out=xsp[:, r, 1, :, :].rearrange("p k n -> p (k n)"), in0=ps[:, XB, 0:D],
                                       scalar=yscale[:, 0:1], in1=xsp[:, r, 0, :, :].rearrange("p k n -> p (k n)"),
                                       op0=ALU.mult, op1=ALU.subtract).then_inc(x_split, 1)

            def split_h(j, u):
                for gg in range(2):
                    n = (2 * u + gg) % NH
                    hi, lo = (hsp[:, n, s, :, :].rearrange("p c n -> p (c n)") for s in range(2))
                    s_h = cur[:, u % RING, C_H:C_H + 1]
                    if gg == 0:
                        dve.wait_ge(x_split, j + 1)
                    dve.wait_ge(gelu_done, 2 * j + gg + 1)
                    v.tensor_scalar(hi, h32[:, gg, :], s_h, None, ALU.mult).then_inc(h_hi, 1)
                    dve.wait_ge(h_hi, 2 * j + gg + 1)
                    v.scalar_tensor_tensor(out=lo, in0=h32[:, gg, :], scalar=s_h, in1=hi,
                                           op0=ALU.mult, op1=ALU.subtract).then_inc(h_split, 1)

            def rows_out(j, u):
                e = expert_of(dve, j)
                r = u % RING
                dve.wait_ge(l2_done, j + 1)
                if not (isinstance(j, int) and j < RING):
                    dve.wait_ge(added, 16 * (j - RING + 1))
                v.scalar_tensor_tensor(out=outb[:, r, :], in0=ps[:, OB + r, 0:D], scalar=cur[:, r, C_O:C_O + 1],
                                       in1=b2bc[:, bass.ds(e, 1), :].rearrange("p a d -> p (a d)"),
                                       op0=ALU.mult, op1=ALU.add).then_inc(o_read, 1)
                dve.wait_ge(o_read, j + 1)
                v.tensor_scalar(outb[:, r, :], outb[:, r, :], cur[:, r, C_P:NCUR], None, ALU.mult).then_inc(o_ready, 1)

            dve.wait_ge(y_written, 16)
            dve.wait_ge(b2_in, 16)
            split_x(0, 0)
            split_x(1, 1)
            split_h(0, 0)
            for u in range(RING):
                split_x(u + 2, u + 2)
                split_h(u + 1, u + 1)
                rows_out(u, u)
            with dve.Fori(1, NT // RING - 1) as i:
                for u in range(RING):
                    split_x(RING * i + u + 2, u + 2)
                    split_h(RING * i + u + 1, u + 1)
                    rows_out(RING * i + u, u)
            split_x(NT - 1, 2)
            split_h(NT - 2, 1)
            rows_out(NT - 3, 0)
            split_h(NT - 1, 2)
            rows_out(NT - 2, 1)
            rows_out(NT - 1, 2)


_INS = ["x", "cond_1024", "L0_cond_weight", "L0_ffn_router_w", "L0_ffn_router_b", "L0_ffn_lang_w", "L0_ffn_lang_b",
        "L0_ffn_w1", "L0_ffn_b1", "L0_ffn_w2", "L0_ffn_b2"]


def kernel(**inputs):
    import numpy as _np
    import concourse.bacc as _bacc
    from concourse import mybir as _mybir
    from concourse.bass_utils import run_bass_kernel_spmd as _run

    nc = _bacc.Bacc("TRN2", target_bir_lowering=False, num_devices=1)
    arrays, args = {}, []
    for name in _INS:
        a = _np.ascontiguousarray(inputs[name])
        arrays[f"in_{name}"] = a
        args.append(nc.dram_tensor(f"in_{name}", a.shape, _mybir.dt.from_np(a.dtype), kind="ExternalInput").ap())
    args.append(nc.dram_tensor("out_0", (N + P, D), _mybir.dt.float32, kind="ExternalOutput").ap())
    adaln_moe(nc, *args)
    r = _run(nc, [arrays], core_ids=[0])
    return r.results[0]["out_0"][0:N].reshape(NB, SEQ, D)
```

```python
from contextlib import ExitStack

import concourse.bass as bass
from concourse import mybir

F32, F16, I32, U32 = mybir.dt.float32, mybir.dt.float16, mybir.dt.int32, mybir.dt.uint32
ALU, ACT, AX = mybir.AluOpType, mybir.ActivationFunctionType, mybir.AxisListType
ON_PE, ON_DVE = mybir.EngineType.PE, mybir.EngineType.DVE
RED = bass.bass_isa.ReduceOp

P = 128
NB, SEQ, D = 2, 1024, 256
E, L, F = 8, 4, 1024
NR = E + L
N = NB * SEQ
T = N // P
TB = T // NB
K = 2
NT = N * K // P + E - 1
KD, KF = D // P, F // P
GH = KF // 2
ROW = D + E
EPS = 1e-8
HALF = KD * F
SLOTS = 4
RING = 3
LAST = NT // RING - 1
HI_ACT = range(4, 7)
EARLY = 3
GAP = 6
PEELED = 2
BODY = 5
RANKS_AT = 8
XB3 = 3
YB = (4, 5, 6, 1)
NH = 2 * RING
BIG = 1e30

FIELD_SCALE = 268 - 64
FIELD_GELU = 27
FIELD_MAX = 254
ULP = float(1 << 23)
ROUND = 1.5 * ULP
FIELD_H = 389 - 128
FIELD_HB = 267
FIELD_O = 113 + 64

C_GELU, C_H, C_O, C_P, NCUR = KF, KF + 1, KF + 2, KF + 3, KF + 4


def adaln_moe(nc, x, cond, cw, rw, rb, lw, lb, w1, b1, w2, b2, out):
    y_rows = nc.dram_tensor("y_rows", (N + P, ROW), F32, kind="Internal").ap()
    x_tiles = x.rearrange("b (t p) d -> p (b t) d", p=P)
    w1_v = w1.rearrange("e (k p) f -> e p k f", p=P)
    w2_v = w2.rearrange("e (c p) d -> e p c d", p=P)

    ctx = ExitStack()
    with ctx:
        def sb(name, shape, dt=F32):
            return ctx.enter_context(nc.sbuf_tensor(name, shape, dt))

        def sem(name):
            return ctx.enter_context(nc.semaphore(name))

        wsp = sb("wsp", [P, E, 4 * HALF], F16)
        stage = sb("stage", [P, SLOTS, HALF])
        pay = sb("pay", [P, T * ROW])
        onehot = sb("onehot", [P, K * T * P], F16)
        b2bc = sb("b2bc", [P, E, D])
        tilehot = sb("tilehot", [P, K * T, NT], F16)
        rows = sb("rows", [P, RING, ROW])
        scratch = wsp[:, E - 2, :].bitcast(F32)
        xin = wsp[:, E - 1, :].bitcast(F32).rearrange("p (t d) -> p t d", t=T)
        at = [0]

        def carve(n):
            at[0] += n
            assert at[0] <= 2 * HALF
            return scratch[:, at[0] - n:at[0]]

        W = carve(KD * D).rearrange("p (k d) -> p k d", k=KD)
        WT = carve(KD * D).rearrange("p (o i) -> p o i", o=KD)
        Wsq = carve(KD * D).rearrange("p (k d) -> p k d", k=KD)
        Wy = carve(NB * KD * D).rearrange("p (b k n) -> p b k n", b=NB, k=KD)
        Wr = carve(NB * KD * NR).rearrange("p (b k n) -> p b k n", b=NB, k=KD)
        xT = pay[:, :].rearrange("p (t r) -> p t r", t=T)[:, :, 0:D]
        ident = sb("ident", [P, P])
        tri = sb("tri", [P, P], F16)
        ones = sb("ones", [P, P], F16)
        iota = sb("iota", [P, P], I32)
        first = sb("first", [P, E], I32)
        home = sb("home", [P, E], I32)
        tok1 = sb("tok1", [P, T], I32)
        padi = sb("padi", [P, 1], I32)
        padf = sb("padf", [P, 1])
        tiles_i = sb("tiles_i", [1, NT - E, E], I32)
        te = sb("te", [1, NT], I32)
        condr = sb("condr", [NB * KD, P])
        ys = sb("ys", [P, KD, NB])
        ysq = sb("ysq", [P, KD, NB])
        RL = sb("RL", [NR, D])
        biasr = sb("biasr", [P, NR])
        R = sb("R", [P, KD, NR])
        Rd = sb("Rd", [P, KD, NB, NR])
        dv = sb("dv", [P, 5, KD * NB])
        dcol = sb("dcol", [P, KD, NB])
        b1r = sb("b1r", [E * KF, P])
        tab = sb("tab", [P, E, NCUR])
        cur = sb("cur", [P, RING, NCUR])
        wsum = sb("wsum", [P, 2 * E])
        wmax = sb("wmax", [P, 2 * E])
        wround = sb("wround", [P, 2 * E])
        wt = sb("wt", [P, 2 * E])
        wscale = sb("wscale", [P, 2 * E])
        ysum = sb("ysum", [P, T // 4])
        ysm = sb("ysm", [P, 1])
        ymax = sb("ymax", [P, 1])
        yt = sb("yt", [P, 1], I32)
        yscale = sb("yscale", [P, 1])
        bmx = sb("bmx", [P, E])
        bmax = sb("bmax", [P, E])
        bfield = sb("bfield", [P, E], I32)
        fld = sb("fld", [P, 2, E])
        nfb = sb("nfb", [P, E])
        yg = sb("yg", [P, 2])
        s1 = sb("s1", [P, 8, T])
        M16 = sb("M16", [P, T, E], F16)
        Mt = sb("Mt", [P, E], F16)
        tl = sb("tl", [P, 4, L + E])
        base = sb("base", [P, 3, E])
        tli = sb("tli", [P, 2, E], I32)
        cmp = sb("cmp", [1, NT - E, E])
        tef = sb("tef", [1, NT - E])
        slot = sb("slot", [P, K, T])
        sloti = sb("sloti", [P, 3, K * T], I32)
        idx = sb("idx", [P, NT], U32)
        padv = sb("padv", [P, NT])
        warm = sb("warm", [P, 1])

        route_at = [0]

        def share(*shape):
            n = 1
            for q in shape:
                n *= q
            route_at[0] += n
            assert route_at[0] <= E * D
            flat = b2bc[:, :, :].rearrange("p e d -> p (e d)")[:, route_at[0] - n:route_at[0]]
            return flat.rearrange("p (t e) -> p t e", t=shape[0]) if len(shape) == 2 else flat.rearrange(
                "p (k t e) -> p k t e", k=shape[0], t=shape[1])

        lg, lpp, le = share(T, NR), share(T, L + 1), share(T, L)
        eq, r2, oh = share(T, E), share(T, E), share(K, T, E)

        payv = pay[:, :].rearrange("p (t r) -> p t r", t=T)
        h32 = pay[:, 0:2 * GH * P].rearrange("p (g n) -> p g n", g=2)
        hsp = pay[:, 2 * GH * P:2 * GH * P + NH * GH * P].bitcast(F16).rearrange(
            "p (h s c n) -> p h s c n", h=NH, s=2, c=GH)
        ohv = onehot[:, :].rearrange("p (c s) -> p c s", s=P)
        xsp = onehot[:, 0:RING * 2 * D].rearrange("p (r s k n) -> p r s k n", r=RING, s=2, k=KD)
        outb = onehot[:, RING * 2 * D:RING * 4 * D].bitcast(F32).rearrange("p (r n) -> p r n", r=RING)

        ps = ctx.enter_context(nc.psum_tensor("ps", [P, 8, 512], F32))
        HB, OB, XB, MB = 0, 3, 6, 7

        consts = sem("consts"); small_in = sem("small_in"); cond_in = sem("cond_in"); cw_in = sem("cw_in"); x_in = [sem(f"x_in{c}") for c in range(4)]
        w_in = [sem(f"w_in{i}") for i in range(SLOTS)]
        b2_in = sem("b2_in"); pads_out = sem("pads_out"); x_copied = sem("x_copied"); y_written = sem("y_written")
        zero_ready = sem("zero_ready")
        cond_psum = sem("cond_psum"); wr_ready = sem("wr_ready"); lg_psum = sem("lg_psum"); lg_read = sem("lg_read")
        warm_ready = sem("warm_ready"); pool_step = sem("pool_step"); cur_ready = sem("cur_ready")
        wt_psum = sem("wt_psum"); wt_ready = sem("wt_ready"); rb_psum = sem("rb_psum")
        sq_ready = sem("sq_ready"); v_psum = sem("v_psum"); v_ready = sem("v_ready"); v_root = sem("v_root")
        d_ready = sem("d_ready"); rd_ready = sem("rd_ready"); d_psum = sem("d_psum"); wr_psum = sem("wr_psum")
        wp_ready = sem("wp_ready"); b1_ready = sem("b1_ready"); b1_max = sem("b1_max")
        xt_psum = sem("xt_psum"); xt_ready = sem("xt_ready"); y_psum = sem("y_psum"); y_ready = sem("y_ready")
        y_sq = sem("y_sq"); ym_ready = sem("ym_ready"); y_max = sem("y_max")
        lang_in = sem("lang_in"); lang_exp = sem("lang_exp"); gap_in = sem("gap_in"); gap_exp = sem("gap_exp")
        picked = sem("picked"); p_ready = sem("p_ready"); counted = sem("counted"); ranked = sem("ranked"); hot_ready = sem("hot_ready")
        mapped = sem("mapped"); idx_ready = sem("idx_ready"); te_ready = sem("te_ready")
        w_sq = sem("w_sq"); w_max = sem("w_max"); w_scaled = sem("w_scaled"); w_t = sem("w_t"); w_hi_pool = sem("w_hi_pool"); w_hi_act = sem("w_hi_act"); w_split = sem("w_split")
        tab_ready = sem("tab_ready")
        dve_step = sem("dve_step")
        gathered = [sem(f"gathered{r}") for r in range(RING)]
        t_done = sem("t_done"); ys_ready = sem("ys_ready"); x_hi = sem("x_hi"); x_split = sem("x_split")
        l1_done = sem("l1_done"); gelu_done = sem("gelu_done"); h_hi = sem("h_hi"); h_split = sem("h_split")
        l2_done = sem("l2_done"); o_sum = sem("o_sum"); o_read = sem("o_read"); o_ready = sem("o_ready"); added = sem("added")

        def parts_of(n):
            e = n // 2
            if n % 2 == 0:
                return [wsp[:, e, s * HALF:(s + 1) * HALF].rearrange("p (c d) -> p c d", d=D) for s in range(2)]
            both = wsp[:, e, 2 * HALF:4 * HALF].rearrange("p (c s d) -> p c s d", c=KF, s=2)
            return [both[:, :, s, :] for s in range(2)]

        def wait_hi(eng, n):
            if n in HI_ACT:
                eng.wait_ge(w_hi_act, n - HI_ACT[0] + 1)
            else:
                eng.wait_ge(w_hi_pool, n + 1 - (len(HI_ACT) if n > HI_ACT[0] else 0))

        def wait_split(eng, n):
            eng.wait_ge(w_split, n + 1)

        def staged(n):
            return stage[:, n % SLOTS, :].rearrange("p (c d) -> p c d", d=D)

        def experts_of(engine, j, n):
            _, values = nc.values_load_multi_w_load_instructions(
                te[0:1, bass.ds(j, n)], engines=(engine,), min_val=0, max_val=E - 1,
                skip_runtime_bounds_check_because="te counts experts and is cut off at the last one")
            return values

        def expert_of(engine, j):
            return j if isinstance(j, int) and j < E else experts_of(engine, j, 1)[0]

        block = ctx.enter_context(nc.Block())

        @block.sync
        def _(sp):
            sp.dma_start(condr[:, :], cond.rearrange("b (k p) -> (b k) p", p=P)).then_inc(cond_in, 16)
            sp.dma_start(W, cw.rearrange("(k p) d -> p k d", p=P)).then_inc(cw_in, 16)

            def load_x(c):
                sp.dma_start(xin[:, 4 * c:4 * c + 4, :], x_tiles[:, 4 * c:4 * c + 4, :]).then_inc(x_in[c], 16)

            load_x(0)
            sp.dma_start(RL[0:E, :], rw).then_inc(small_in, 16)
            sp.dma_start(RL[E:NR, :], lw).then_inc(small_in, 16)
            sp.dma_start(b1r[:, :], b1.rearrange("e (c p) -> (e c) p", p=P)).then_inc(small_in, 16)
            sp.dma_start(biasr[:, 0:E], rb.rearrange("(a n) -> a n", a=1).broadcast_to([P, E])).then_inc(small_in, 16)
            sp.dma_start(biasr[:, E:NR], lb.rearrange("(a n) -> a n", a=1).broadcast_to([P, L])).then_inc(small_in, 16)

            def load_weights(n):
                if n >= SLOTS:
                    wait_split(sp, n - SLOTS)
                src = (w1_v if n % 2 == 0 else w2_v)[n // 2]
                dst = stage[:, n % SLOTS, :].rearrange("p (k f) -> p k f", k=KD if n % 2 == 0 else KF)
                sp.dma_start(dst, src).then_inc(w_in[n % SLOTS], 16)

            load_weights(0)
            load_x(1)
            load_weights(1)
            load_x(2)
            load_x(3)
            for n in range(2, SLOTS):
                load_weights(n)
            sp.wait_ge(zero_ready, 1)
            sp.dma_start(y_rows[N:N + P, :], rows[:, 0, :]).then_inc(pads_out, 16)
            sp.dma_start(out[N:N + P, :], rows[:, 0, 0:D]).then_inc(pads_out, 16)
            for n in range(SLOTS, SLOTS + EARLY):
                load_weights(n)
            sp.dma_start(out[0:N, :], x.rearrange("b s d -> (b s) d")).then_inc(x_copied, 16)
            sp.wait_ge(p_ready, 1)
            for c in range(4):
                sp.wait_ge(y_ready, 4 * c + 4)
                sp.dma_start(y_rows[0:N, :].rearrange("(t p) r -> p t r", p=P)[:, 4 * c:4 * c + 4, :],
                             payv[:, 4 * c:4 * c + 4, :]).then_inc(y_written, 16)
            for n in range(SLOTS + EARLY, 2 * SLOTS + 2):
                load_weights(n)
            sp.wait_ge(idx_ready, 1)
            sp.dma_start(b2bc[:, :, :].rearrange("p e d -> p (e d)"),
                         b2.rearrange("(a e) d -> a (e d)", a=1).broadcast_to([P, E * D])).then_inc(b2_in, 16)
            for n in range(2 * SLOTS + 2, 2 * E):
                load_weights(n)

        @block.gpsimd
        def _(pool):
            g = nc.gpsimd
            g.memset(warm[:, :], 0.0).then_inc(warm_ready, 1)
            g.memset(ident[:, :], 0.0).then_inc(consts, 1)
            g.memset(tri[:, :], 1.0).then_inc(consts, 1)
            g.memset(ones[:, :], 1.0).then_inc(consts, 1)
            g.iota(iota[:, :], pattern=[[1, P]], base=0, channel_multiplier=0).then_inc(consts, 1)
            g.iota(first[:, :], pattern=[[-1, E]], base=E, channel_multiplier=0).then_inc(consts, 1)
            g.iota(home[:, :], pattern=[[P, E]], base=0, channel_multiplier=0).then_inc(consts, 1)
            g.iota(tok1[:, :], pattern=[[P, T]], base=1, channel_multiplier=1).then_inc(consts, 1)
            g.iota(padi[:, :], pattern=[[0, 1]], base=N + 1, channel_multiplier=1).then_inc(consts, 1)
            g.iota(tiles_i[:, :, :], pattern=[[1, NT - E], [0, E]], base=0, channel_multiplier=0).then_inc(consts, 1)
            g.iota(te[:, 0:E], pattern=[[1, E]], base=0, channel_multiplier=0).then_inc(consts, 1)
            g.memset(lpp[:, :, L:L + 1], 0.0).then_inc(consts, 1)
            g.memset(tl[:, :, 0:L], 0.0).then_inc(consts, 1)
            g.memset(rows[:, 0, :], 0.0).then_inc(zero_ready, 1)
            pool.wait_ge(consts, 12)
            g.affine_select(out=ident[:, :], in_=ident[:, :], compare_op=ALU.not_equal, fill=1.0, base=0,
                            pattern=[[-1, P]], channel_multiplier=1).then_inc(consts, 1)
            g.affine_select(out=tri[:, :], in_=tri[:, :], compare_op=ALU.is_gt, fill=0.0, base=0,
                            pattern=[[1, P]], channel_multiplier=-1).then_inc(consts, 1)
            g.tensor_copy(padf[:, :], padi[:, :]).then_inc(consts, 1)

            psteps = [0]

            def step(ins):
                psteps[0] += 1
                ins.then_inc(pool_step, 1)
                pool.wait_ge(pool_step, psteps[0])

            def scale_weights(n):
                pool.wait_ge(w_sq, n + 1)
                step(g.partition_all_reduce(wmax[:, n:n + 1], wsum[:, n:n + 1], P, RED.max))
                step(g.tensor_scalar(wround[:, n:n + 1], wmax[:, n:n + 1].bitcast(I32), 2.0 ** -24, ROUND,
                                     ALU.mult, ALU.add))
                g.tensor_scalar(wscale[:, n:n + 1].bitcast(I32), wround[:, n:n + 1], -ULP,
                                (FIELD_SCALE + 1 + ROUND) * ULP, ALU.mult, ALU.add).then_inc(w_scaled, 1)
                g.tensor_scalar(wt[:, n:n + 1], wround[:, n:n + 1], -(ROUND + 1), 1.0, ALU.add, ALU.mult).then_inc(w_t, 1)

            def split_hi(n):
                if n == 2 * (E - 2):
                    pool.wait_ge(y_psum, T)
                pool.wait_ge(w_scaled, n + 1)
                g.tensor_scalar(parts_of(n)[0], staged(n), wscale[:, n:n + 1], 1.0,
                                ALU.mult, ALU.mult).then_inc(w_hi_pool, 1)

            pool.wait_ge(b1_ready, 1)
            g.partition_all_reduce(bmax[:, :], bmx[:, :], P, RED.max).then_inc(b1_max, 1)
            for n in range(HI_ACT[0]):
                scale_weights(n)
                split_hi(n)
            for n in (4, 5, 6):
                scale_weights(n)

            def gather(j):
                g.indirect_dma_start(out=rows[:, j % RING, :], out_offset=None, in_=y_rows,
                                     in_offset=bass.IndirectOffsetOnAxis(ap=idx[:, j:j + 1], axis=0)
                                     ).then_inc(gathered[j % RING], 16)

            pool.wait_ge(y_written, 16 * 4)
            pool.wait_ge(pads_out, 32)
            pool.wait_ge(idx_ready, 1)
            for j in range(RING):
                gather(j)
            pool.wait_ge(ym_ready, 1)
            g.partition_all_reduce(ymax[:, :], ysm[:, :], P, RED.max).then_inc(y_max, 1)
            for j in range(NT):
                for q in ([RING, RING + 1] if j == 0 else [j + RING + 1]):
                    if q < NT:
                        pool.wait_ge(cur_ready, q - RING + 1)
                        gather(q)
                for n in range(GAP + (2 * j + 2 if j else 1), min(GAP + 2 * j + 4, 2 * E)):
                    scale_weights(n)
                    split_hi(n)
                if j == 0:
                    pool.wait_ge(x_copied, 16)
                pool.wait_ge(o_ready, j + 1)
                if j:
                    pool.wait_ge(added, 16 * j)
                g.indirect_dma_start(out=out, out_offset=bass.IndirectOffsetOnAxis(ap=idx[:, j:j + 1], axis=0),
                                     in_=outb[:, j % RING, :], in_offset=None,
                                     compute_op=ALU.add).then_inc(added, 16)
            pool.wait_ge(added, 16 * NT)

        @block.tensor
        def _(pe):
            mm, tr = nc.tensor.matmul, nc.tensor.transpose
            pe.wait_ge(consts, 15)
            pe.wait_ge(cond_in, 16)
            tr(ps[:, 7, 0:NB * KD], condr[:, :], ident[0:NB * KD, 0:NB * KD]).then_inc(cond_psum, 1)
            pe.wait_ge(cw_in, 16)
            for o in range(KD):
                for k in range(KD):
                    last = tr(ps[:, 0, (o * KD + k) * P:(o * KD + k + 1) * P], W[:, k, o * P:(o + 1) * P], ident[:, :])
            last.then_inc(wt_psum, 1)
            pe.wait_ge(sq_ready, 1)
            for o in range(KD):
                for k in range(KD):
                    last = mm(ps[:, 2, o * NB:(o + 1) * NB], Wsq[:, k, o * P:(o + 1) * P], ysq[:, k, :],
                              start=(k == 0), stop=(k == KD - 1))
            last.then_inc(v_psum, 1)
            pe.wait_ge(small_in, 16 * 5)
            for k in range(KD):
                tr(ps[:, 1, k * NR:(k + 1) * NR], RL[:, k * P:(k + 1) * P], ident[0:NR, 0:NR])
            tr(ps[:, 1, 64:64 + E * KF], b1r[:, :], ident[0:E * KF, 0:E * KF]).then_inc(rb_psum, 1)

            def transpose_x(q):
                if q % 2 == 0:
                    pe.wait_ge(x_in[q // 2], 16)
                if q >= XB3:
                    pe.wait_ge(xt_ready, q - XB3 + 1)
                for t in range(2):
                    for k in range(KD):
                        last = tr(ps[:, 5 + q % XB3, (t * KD + k) * P:(t * KD + k + 1) * P],
                                  xin[:, 2 * q + t, k * P:(k + 1) * P], ident[:, :])
                last.then_inc(xt_psum, 1)

            transpose_x(0)
            pe.wait_ge(rd_ready, 1)
            pe.wait_ge(wt_ready, 1)
            for k in range(KD):
                for o in range(KD):
                    last = mm(ps[:, 4, k * NB * NR:(k + 1) * NB * NR], WT[:, o, k * P:(k + 1) * P],
                              Rd[:, o, :, :].rearrange("p b n -> p (b n)"), start=(o == 0), stop=(o == KD - 1))
            last.then_inc(wr_psum, 1)
            for b in range(NB):
                for o in range(KD):
                    last = mm(ps[:, 3, b * D + o * P:b * D + (o + 1) * P],
                              dcol[:, o, b:b + 1].broadcast_to([P, P]), ident[:, :], start=True, stop=True)
            last.then_inc(d_psum, 1)
            transpose_x(1)
            pe.wait_ge(wr_ready, 1)
            for q in range(T // 2):
                if q + 2 < T // 2:
                    transpose_x(q + 2)
                pe.wait_ge(xt_ready, q + 1)
                for t in (2 * q, 2 * q + 1):
                    for k in range(KD):
                        last = mm(ps[:, 0, t * NR:(t + 1) * NR], xT[:, t, k * P:(k + 1) * P], Wr[:, t // TB, k, :],
                                  start=(k == 0), stop=(k == KD - 1))
            last.then_inc(lg_psum, 1)

            def rows_of_y(t):
                if t >= 4:
                    pe.wait_ge(y_ready, t - 3)
                for k in range(KD):
                    last = mm(ps[:, YB[t % 4], 0:D], xT[:, t, k * P:(k + 1) * P], Wy[:, t // TB, k, :],
                              start=(k == 0), stop=(k == KD - 1))
                last.then_inc(y_psum, 1)

            pe.wait_ge(wp_ready, 1)
            pe.wait_ge(xt_ready, T // 2)
            for t in range(RANKS_AT):
                rows_of_y(t)
            pe.wait_ge(picked, 1)
            mm(ps[:, 3, 0:E], ones[:, :], Mt[:, :], start=True, stop=True).then_inc(counted, 1)
            mm(ps[:, 2, 0:T * E], tri[:, :], M16[:, :, :].rearrange("p t e -> p (t e)"), start=True, stop=False)
            for t in range(T - 1):
                last = mm(ps[:, 2, (t + 1) * E:T * E].rearrange("p (a e) -> p a e", e=E), ones[:, :],
                          M16[:, t:t + 1, :].broadcast_to([P, T - 1 - t, E]), start=False, stop=(t == T - 2))
            last.then_inc(ranked, 1)
            for t in range(RANKS_AT, T):
                rows_of_y(t)
            pe.wait_ge(hot_ready, 1)
            for c in range(K * T):
                last = mm(ps[:, MB, 0:NT], ohv[:, c, :], tilehot[:, c, :], start=(c == 0), stop=(c == K * T - 1))
            last.then_inc(mapped, 1)
            pe.wait_ge(y_ready, T)

            def transpose_rows(j, i, u):
                pe.wait_ge(gathered[u % RING], 16 * (i + 1 + u // RING))
                if not (isinstance(j, int) and j == 0):
                    pe.wait_ge(x_split, j)
                for k in range(KD):
                    last = tr(ps[:, XB, k * P:(k + 1) * P], rows[:, u % RING, k * P:(k + 1) * P], ident[:, :])
                last.then_inc(t_done, 1)

            def blocks(uj, uu, ue, gg, dj, du, de, dg):
                if uj is not None:
                    if isinstance(uj, int) and uj < E:
                        wait_split(pe, 2 * uj)
                    pe.wait_ge(x_split, uj + 1)
                    if not (isinstance(uj, int) and 2 * uj + gg < RING):
                        pe.wait_ge(gelu_done, 2 * uj + gg - 2)
                if dj is not None:
                    if isinstance(dj, int) and dj < E:
                        wait_split(pe, 2 * dj + 1)
                    if dg == 0 and not (isinstance(dj, int) and dj < RING):
                        pe.wait_ge(o_read, dj - RING + 1)
                    pe.wait_ge(h_split, 2 * dj + dg + 1)
                up_last = down_last = None
                for c in range(GH):
                    if uj is not None:
                        steps = [(0, 0, 0), (0, 0, 1), (0, 1, 0), (0, 1, 1), (1, 0, 0), (1, 1, 0)]
                        for q, (w, k, s) in enumerate(steps):
                            o = w * HALF + k * F + (gg * GH + c) * P
                            up_last = mm(ps[:, HB + (2 * uu + gg) % RING, c * P:(c + 1) * P],
                                         wsp[:, bass.ds(ue, 1), o:o + P].rearrange("p a f -> p (a f)"),
                                         xsp[:, uu % RING, s, k, :], start=(q == 0), stop=(q == len(steps) - 1))
                    if dj is not None:
                        cc = dg * GH + c
                        for s, width in ((0, 2 * D), (1, D)):
                            o = 2 * HALF + cc * 2 * D
                            down_last = mm(ps[:, OB + du % RING, 0:width], hsp[:, (2 * du + dg) % NH, s, c, :],
                                           wsp[:, bass.ds(de, 1), o:o + width].rearrange("p a f -> p (a f)"),
                                           start=(cc == 0 and s == 0), stop=(cc == KF - 1 and s == 1))
                if uj is not None:
                    up_last.then_inc(l1_done, 1)
                if dj is not None and dg == 1:
                    down_last.then_inc(l2_done, 1)

            def turn(j, i, u, e_before, e_now, e_next, first=False, turned=True):
                if turned:
                    transpose_rows(j + 2, i, u + 2)
                down = (None, 0, 0, 0) if first else (j - 1, u - 1 + RING, e_before, 1)
                blocks(j + 1, u + 1, e_next, 0, *down)
                blocks(j + 1, u + 1, e_next, 1, j, u, e_now, 0)

            transpose_rows(0, 0, 0)
            transpose_rows(1, 0, 1)
            for gg in range(2):
                blocks(0, 0, 0, gg, None, 0, 0, 0)
            for j in range(PEELED * RING):
                turn(j, j // RING, j % RING, j - 1, j, j + 1, first=(j == 0))
            pe.wait_ge(te_ready, 1)
            wait_split(pe, 2 * E - 1)
            with pe.Fori(0, (LAST - PEELED) // BODY) as i:
                ring0 = PEELED + BODY * i
                e = experts_of(ON_PE, RING * ring0 - 1, 2)
                for u in range(BODY * RING):
                    if u % RING == 0:
                        e = e[-2:] + experts_of(ON_PE, RING * ring0 + u + 1, RING)
                    turn(RING * ring0 + u, ring0 + u // RING, u % RING, *e[u % RING:u % RING + 3])
            j = RING * LAST
            es = experts_of(ON_PE, j - 1, RING + 1)
            turn(j, LAST, 0, es[0], es[1], es[2])
            turn(j + 1, LAST, 1, es[1], es[2], es[3], turned=False)
            blocks(None, 0, 0, 0, j + 1, 1, es[2], 1)
            for dg in range(2):
                blocks(None, 0, 0, 0, j + 2, 2, es[3], dg)

        @block.scalar
        def _(act):
            a = nc.scalar
            act.wait_ge(warm_ready, 1)
            a.activation(warm[:, :], warm[:, :], ACT.Sqrt)
            act.wait_ge(wt_psum, 1)
            a.activation(WT.rearrange("p o i -> p (o i)"), ps[:, 0, :], ACT.Copy).then_inc(wt_ready, 1)
            act.wait_ge(v_ready, 1)
            a.activation(dv[:, 1, :], dv[:, 0, :], ACT.Sqrt).then_inc(v_root, 1)
            a.activation(ymax[:, :], dv[:, 0, 0:1], ACT.Exp).then_inc(warm_ready, 1)

            def square_weights(n):
                act.wait_ge(w_in[n % SLOTS], 16 * (n // SLOTS + 1))
                if n // 2 >= E - 2:
                    act.wait_ge(y_psum, T)
                a.activation(parts_of(n)[1], staged(n), ACT.Square, accum_out=wsum[:, n:n + 1]).then_inc(w_sq, 1)

            def split_hi(n):
                act.wait_ge(w_scaled, n + 1)
                a.activation(parts_of(n)[0], staged(n), ACT.Copy, scale=wscale[:, n:n + 1]).then_inc(w_hi_act, 1)

            square_weights(0)
            for q in range(T // 2):
                act.wait_ge(xt_psum, q + 1)
                a.activation(xT[:, 2 * q:2 * q + 2, :], ps[:, 5 + q % XB3, :].rearrange("p (t n) -> p t n", t=2),
                             ACT.Copy).then_inc(xt_ready, 1)
                if q == 1:
                    square_weights(1)
                if q == 4:
                    square_weights(2)
                if q == 6:
                    square_weights(3)
            act.wait_ge(lang_in, 1)
            a.activation(le[:, :, :], lpp[:, :, 0:L], ACT.Exp).then_inc(lang_exp, 1)
            for t in range(T):
                act.wait_ge(y_psum, t + 1)
                a.activation(payv[:, t, 0:D], ps[:, YB[t % 4], 0:D], ACT.Copy).then_inc(y_ready, 1)
                if t % 4 == 3:
                    c = t // 4
                    act.wait_ge(y_ready, t + 1)
                    a.activation(xin[:, 4 * c:4 * c + 4, :], payv[:, 4 * c:4 * c + 4, 0:D], ACT.Square,
                                 accum_out=ysum[:, c:c + 1]).then_inc(y_sq, 1)
                if t == 1:
                    square_weights(4)
                if t == 5:
                    act.wait_ge(gap_in, 1)
                    a.activation(s1[:, 5, :], s1[:, 4, :], ACT.Exp).then_inc(gap_exp, 1)
                    split_hi(4)
                if t == 8:
                    square_weights(5)
                if t == 12:
                    split_hi(5)
            square_weights(6)
            split_hi(6)
            a.activation(warm[:, :], s1[:, 4, 0:1], ACT.Gelu)

            def x_high(j, u):
                act.wait_ge(t_done, j + 1)
                a.activation(xsp[:, u % RING, 0, :, :].rearrange("p k n -> p (k n)"), ps[:, XB, 0:D], ACT.Copy,
                             scale=yscale[:, 0:1]).then_inc(x_hi, 1)

            def gelus(j, u, gg):
                n = 2 * (u % RING) + gg
                if gg == 0:
                    act.wait_ge(cur_ready, j + 1)
                act.wait_ge(l1_done, 2 * j + gg + 1)
                if not (isinstance(j, int) and j == 0):
                    act.wait_ge(h_split, 2 * j + gg - 1)
                for c in range(GH):
                    cc = gg * GH + c
                    last = a.activation(h32[:, gg, c * P:(c + 1) * P], ps[:, HB + n % RING, c * P:(c + 1) * P],
                                        ACT.Gelu, bias=cur[:, u % RING, cc:cc + 1],
                                        scale=cur[:, u % RING, C_GELU:C_GELU + 1])
                last.then_inc(gelu_done, 1)
                act.wait_ge(gelu_done, 2 * j + gg + 1)
                a.activation(hsp[:, n, 0, :, :].rearrange("p c n -> p (c n)"), h32[:, gg, :], ACT.Copy,
                             scale=cur[:, u % RING, C_H:C_H + 1]).then_inc(h_hi, 1)

            def weigh(j, u):
                r = u % RING
                act.wait_ge(o_read, j + 1)
                a.activation(outb[:, r, :], outb[:, r, :], ACT.Copy, scale=cur[:, r, C_P:NCUR]).then_inc(o_ready, 1)

            def turn(j, u, first=False, turned=True, squares=()):
                gelus(j, u, 1)
                if turned:
                    x_high(j + 2, u + 2)
                for n in squares[:1]:
                    square_weights(n)
                gelus(j + 1, u + 1, 0)
                if not first:
                    weigh(j - 1, u - 1 + RING)
                for n in squares[1:]:
                    square_weights(n)

            act.wait_ge(ys_ready, 1)
            x_high(0, 0)
            x_high(1, 1)
            gelus(0, 0, 0)
            square_weights(GAP + 1)
            for j in range(PEELED * RING):
                turn(j, j % RING, first=(j == 0), squares=range(GAP + 2 * j + 2, min(GAP + 2 * j + 4, 2 * E)))
            with act.Fori(0, (LAST - PEELED) // BODY) as i:
                for u in range(BODY * RING):
                    turn(RING * (PEELED + BODY * i) + u, u % RING)
            turn(NT - 3, 0)
            turn(NT - 2, 1, turned=False)
            gelus(NT - 1, 2, 1)
            for j in (NT - 2, NT - 1):
                weigh(j, j % RING)

        @block.vector
        def _(dve):
            v = nc.vector
            steps = [0]

            def step(ins):
                steps[0] += 1
                ins.then_inc(dve_step, 1)
                dve.wait_ge(dve_step, steps[0])

            dve.wait_ge(cw_in, 16)
            v.tensor_tensor(Wsq, W, W, ALU.mult)
            dve.wait_ge(cond_psum, 1)
            step(v.tensor_scalar(ys[:, :, :], ps[:, 7, 0:NB * KD].rearrange("p (b k) -> p k b", b=NB), D ** -0.5, None,
                                 ALU.mult))
            v.tensor_tensor(ysq[:, :, :], ys[:, :, :], ys[:, :, :], ALU.mult).then_inc(sq_ready, 1)
            dve.wait_ge(v_psum, 1)
            v.tensor_scalar(dv[:, 0, :], ps[:, 2, 0:KD * NB], EPS, None, ALU.add).then_inc(v_ready, 1)
            dve.wait_ge(rb_psum, 1)
            step(v.tensor_copy(R[:, :, :], ps[:, 1, 0:KD * NR].rearrange("p (k n) -> p k n", k=KD)))
            step(v.tensor_copy(tab[:, :, 0:KF], ps[:, 1, 64:64 + E * KF].rearrange("p (e c) -> p e c", e=E)))
            v.tensor_reduce(bmx[:, :], tab[:, :, 0:KF], AX.X, ALU.max, apply_absolute_value=True).then_inc(b1_ready, 1)
            dve.wait_ge(v_root, 1)
            step(v.reciprocal(dv[:, 2, :], dv[:, 1, :]))
            step(v.tensor_tensor(dv[:, 3, :], dv[:, 2, :], dv[:, 2, :], ALU.mult))
            step(v.tensor_tensor(dv[:, 4, :], dv[:, 3, :], dv[:, 0, :], ALU.mult))
            step(v.tensor_scalar(dv[:, 3, :], dv[:, 4, :], -0.5, 1.5, ALU.mult, ALU.add))
            dve.wait_ge(v_ready, 1)
            v.tensor_tensor(dcol[:, :, :].rearrange("p o b -> p (o b)"), dv[:, 2, :], dv[:, 3, :],
                            ALU.mult).then_inc(d_ready, 1)
            dve.wait_ge(d_ready, 1)
            for b in range(NB):
                last = v.tensor_tensor(Rd[:, :, b, :], R[:, :, :], dcol[:, :, b:b + 1].broadcast_to([P, KD, NR]), ALU.mult)
            last.then_inc(rd_ready, 1)
            dve.wait_ge(wr_psum, 1)
            wr = ps[:, 4, 0:KD * NB * NR].rearrange("p (k b n) -> p b k n", k=KD, b=NB)
            for b in range(NB):
                last = v.tensor_tensor(Wr[:, b, :, :], wr[:, b, :, :], ys[:, :, b:b + 1].broadcast_to([P, KD, NR]), ALU.mult)
            last.then_inc(wr_ready, 1)
            dve.wait_ge(d_psum, 1)
            for b in range(NB):
                for k in range(KD):
                    last = v.scalar_tensor_tensor(out=Wy[:, b, k, :], in0=W[:, k, :], scalar=ys[:, k, b:b + 1],
                                                  in1=ps[:, 3, b * D:(b + 1) * D], op0=ALU.mult, op1=ALU.mult)
            last.then_inc(wp_ready, 1)

            def split_lo(n):
                hi, lo = parts_of(n)
                wait_hi(dve, n)
                v.scalar_tensor_tensor(out=lo, in0=staged(n), scalar=wscale[:, n:n + 1], in1=hi,
                                       op0=ALU.mult, op1=ALU.subtract).then_inc(w_split, 1)

            for n in range(EARLY):
                split_lo(n)
            dve.wait_ge(lg_psum, 1)
            v.tensor_tensor(lg[:, :, :], ps[:, 0, 0:T * NR].rearrange("p (t n) -> p t n", t=T),
                            biasr[:, :].rearrange("p (a n) -> p a n", a=1).broadcast_to([P, T, NR]),
                            ALU.add).then_inc(lg_read, 1)

            lang, route = lg[:, :, E:NR], lg[:, :, 0:E]

            def over(ap, n):
                return ap.rearrange("p (t a) -> p t a", a=1).broadcast_to([P, T, n])

            dve.wait_ge(lg_read, 1)
            step(v.tensor_reduce(s1[:, 0, :], lang, AX.X, ALU.max))
            v.tensor_tensor(lpp[:, :, 0:L], lang, over(s1[:, 0, :], L), ALU.subtract).then_inc(lang_in, 1)
            dve.wait_ge(lang_exp, 1)
            step(v.tensor_reduce(s1[:, 1, :], le[:, :, :], AX.X, ALU.add))
            step(v.reciprocal(s1[:, 2, :], s1[:, 1, :]))
            step(v.tensor_tensor(lpp[:, :, 0:L], le[:, :, :], over(s1[:, 2, :], L), ALU.mult))
            step(v.tensor_tensor(le[:, :, :], lpp[:, :, 0:L], lpp[:, :, 1:L + 1], ALU.add))
            for q in range(E // L):
                last = v.scalar_tensor_tensor(out=route[:, :, q * L:(q + 1) * L], in0=le[:, :, :], scalar=0.1,
                                              in1=route[:, :, q * L:(q + 1) * L], op0=ALU.mult, op1=ALU.add)
            step(last)

            def pick(k, logits, m):
                step(v.tensor_reduce(s1[:, m, :], logits, AX.X, ALU.max))
                step(v.tensor_tensor(eq[:, :, :], logits, over(s1[:, m, :], E), ALU.is_equal))
                step(v.tensor_tensor(eq[:, :, :], eq[:, :, :],
                                     first[:, :].rearrange("p (a e) -> p a e", a=1).broadcast_to([P, T, E]), ALU.mult))
                step(v.tensor_reduce(s1[:, 3, :], eq[:, :, :], AX.X, ALU.max))
                step(v.tensor_tensor(oh[:, k, :, :], eq[:, :, :], over(s1[:, 3, :], E), ALU.is_equal))

            pick(0, route, 6)
            step(v.scalar_tensor_tensor(out=r2[:, :, :], in0=oh[:, 0, :, :], scalar=-BIG, in1=route,
                                        op0=ALU.mult, op1=ALU.add))
            pick(1, r2[:, :, :], 7)
            step(v.tensor_tensor(M16[:, :, :], oh[:, 0, :, :], oh[:, 1, :, :], ALU.add))
            with nc.allow_low_precision(reason="counts of at most 16"):
                v.tensor_reduce(Mt[:, :], M16[:, :, :].rearrange("p t e -> p e t"), AX.X, ALU.add).then_inc(picked, 1)
            v.tensor_tensor(s1[:, 4, :], s1[:, 7, :], s1[:, 6, :], ALU.subtract).then_inc(gap_in, 1)
            dve.wait_ge(gap_exp, 1)
            step(v.tensor_scalar(s1[:, 0, :], s1[:, 5, :], 1.0, None, ALU.add))
            step(v.reciprocal(s1[:, 1, :], s1[:, 0, :]))
            step(v.tensor_tensor(s1[:, 2, :], s1[:, 5, :], s1[:, 1, :], ALU.mult))
            step(v.tensor_tensor(eq[:, :, :], oh[:, 0, :, :], over(s1[:, 1, :], E), ALU.mult))
            step(v.tensor_tensor(r2[:, :, :], oh[:, 1, :, :], over(s1[:, 2, :], E), ALU.mult))
            v.tensor_tensor(payv[:, :, D:ROW], eq[:, :, :], r2[:, :, :], ALU.add).then_inc(p_ready, 1)

            dve.wait_ge(counted, 1)
            step(v.tensor_scalar(tli[:, 0, :], ps[:, 3, 0:E], float(P - 1), None, ALU.add))
            step(v.tensor_scalar(tli[:, 1, :], tli[:, 0, :], 7, None, ALU.logical_shift_right))
            step(v.tensor_scalar(tl[:, 0, L:], tli[:, 1, :], -1.0, 0.0, ALU.add, ALU.max))
            for q, d in enumerate((1, 2, 4)):
                step(v.tensor_tensor(tl[:, q + 1, L:], tl[:, q, L:], tl[:, q, L - d:L + E - d], ALU.add))
            ends = tl[:, 3, L:]
            step(v.tensor_tensor(base[:, 0, :], ends, tl[:, 0, L:], ALU.subtract))
            step(v.tensor_scalar(base[:, 1, :], base[:, 0, :], float(P), float((E - 1) * P), ALU.mult, ALU.add))
            step(v.tensor_tensor(base[:, 2, :], base[:, 1, :], home[:, :], ALU.subtract))
            rank = ps[:, 2, 0:T * E].rearrange("p (t e) -> p t e", e=E)

            def each(ap):
                return ap.rearrange("p (a e) -> p a e", a=1).broadcast_to([P, T, E])

            dve.wait_ge(p_ready, 1)
            dve.wait_ge(ranked, 1)
            step(v.scalar_tensor_tensor(out=eq[:, :, :], in0=rank, scalar=float(P), in1=each(base[:, 2, :]),
                                        op0=ALU.is_ge, op1=ALU.mult))
            step(v.tensor_tensor(r2[:, :, :], rank, eq[:, :, :], ALU.add))
            step(v.tensor_tensor(eq[:, :, :], r2[:, :, :], each(home[:, :]), ALU.add))
            for k in range(K):
                step(v.tensor_tensor(r2[:, :, :], oh[:, k, :, :], eq[:, :, :], ALU.mult))
                step(v.tensor_reduce(slot[:, k, :], r2[:, :, :], AX.X, ALU.add))
            step(v.tensor_copy(sloti[:, 0, :], slot[:, :, :].rearrange("p k t -> p (k t)")))
            step(v.tensor_scalar(sloti[:, 2, :], sloti[:, 0, :], P - 1, None, ALU.bitwise_and))
            step(v.tensor_scalar(sloti[:, 1, :], sloti[:, 0, :], 7, None, ALU.logical_shift_right))
            for k in range(K):
                c = slice(k * T, (k + 1) * T)
                v.tensor_tensor(ohv[:, c, :], iota[:, :].rearrange("p (a n) -> p a n", a=1).broadcast_to([P, T, P]),
                                over(sloti[:, 2, c], P), ALU.is_equal)
            for k in range(K):
                c = slice(k * T, (k + 1) * T)
                step(v.tensor_tensor(tilehot[:, c, :],
                                     iota[:, 0:NT].rearrange("p (a n) -> p a n", a=1).broadcast_to([P, T, NT]),
                                     over(sloti[:, 1, c], NT), ALU.is_equal))
            for k in range(K):
                c = slice(k * T, (k + 1) * T)
                last = v.tensor_tensor(tilehot[:, c, :], tilehot[:, c, :], over(tok1[:, :], NT), ALU.mult)
            last.then_inc(hot_ready, 1)

            step(v.tensor_tensor(cmp[:, :, :], tiles_i[:, :, :],
                                 tl[0:1, 3:4, L:].broadcast_to([1, NT - E, E]), ALU.is_ge))
            step(v.tensor_reduce(tef[:, :], cmp[:, :, :], AX.X, ALU.add))
            v.tensor_scalar(te[:, E:NT], tef[:, :], float(E - 1), None, ALU.min).then_inc(te_ready, 1)
            dve.wait_ge(b1_max, 1)
            step(v.tensor_scalar(bfield[:, :], bmax[:, :].bitcast(I32), 23, None, ALU.logical_shift_right))
            step(v.tensor_scalar(nfb[:, :], bfield[:, :], -float(FIELD_HB), -float(FIELD_MAX), ALU.add, ALU.max))
            dve.wait_ge(mapped, 1)
            step(v.tensor_scalar(padv[:, :], ps[:, MB, 0:NT], 0.0, padf[:, 0:1], ALU.is_equal, ALU.mult))
            v.scalar_tensor_tensor(out=idx[:, :], in0=ps[:, MB, 0:NT], scalar=-1.0, in1=padv[:, :],
                                   op0=ALU.add, op1=ALU.add).then_inc(idx_ready, 1)
            split_lo(3)
            dve.wait_ge(y_sq, 4)
            v.tensor_reduce(ysm[:, :], ysum[:, :], AX.X, ALU.max).then_inc(ym_ready, 1)
            dve.wait_ge(y_max, 1)
            step(v.tensor_scalar(yt[:, :], ymax[:, :].bitcast(I32), 24, None, ALU.logical_shift_right))
            v.tensor_scalar(yscale[:, :].bitcast(I32), yt[:, :], -ULP, FIELD_SCALE * ULP, ALU.mult,
                            ALU.add).then_inc(ys_ready, 1)
            v.tensor_scalar(yg[:, 0:1], yt[:, :], -float(FIELD_GELU), None, ALU.add)
            step(v.tensor_scalar(yg[:, 1:2], yt[:, :], -1.0, float(FIELD_H), ALU.mult, ALU.add))
            wt2 = wt[:, :].rearrange("p (e w) -> p e w", w=2)

            def tables(e0, e1):
                dve.wait_ge(w_t, 2 * e1)
                t1, t2 = wt2[:, e0:e1, 0], wt2[:, e0:e1, 1]
                v.tensor_scalar(tab[:, e0:e1, C_GELU].bitcast(I32), t1, yg[:, 0:1], ULP, ALU.add, ALU.mult)
                step(v.scalar_tensor_tensor(out=fld[:, 0, e0:e1], in0=t1, scalar=yg[:, 1:2], in1=nfb[:, e0:e1],
                                            op0=ALU.subtract, op1=ALU.max))
                v.tensor_scalar(tab[:, e0:e1, C_H].bitcast(I32), fld[:, 0, e0:e1], -ULP, None, ALU.mult)
                step(v.scalar_tensor_tensor(out=fld[:, 1, e0:e1], in0=t2, scalar=float(FIELD_O), in1=fld[:, 0, e0:e1],
                                            op0=ALU.add, op1=ALU.add))
                step(v.tensor_scalar(tab[:, e0:e1, C_O].bitcast(I32), fld[:, 1, e0:e1], 1.0, ULP, ALU.max, ALU.mult))

            tables(0, 3)

            def split_x(j, u):
                r = u % RING
                dve.wait_ge(x_hi, j + 1)
                v.scalar_tensor_tensor(out=xsp[:, r, 1, :, :].rearrange("p k n -> p (k n)"), in0=ps[:, XB, 0:D],
                                       scalar=yscale[:, 0:1], in1=xsp[:, r, 0, :, :].rearrange("p k n -> p (k n)"),
                                       op0=ALU.mult, op1=ALU.subtract).then_inc(x_split, 1)

            def expert_table(j, u, e):
                r = u % RING
                if not (isinstance(j, int) and j < RING):
                    dve.wait_ge(o_ready, j - RING + 1)
                v.tensor_copy(cur[:, r, 0:C_P], tab[:, bass.ds(e, 1), 0:C_P].rearrange("p a c -> p (a c)"))
                v.tensor_copy(cur[:, r, C_P:NCUR], rows[:, r, bass.ds(e + D, 1)]).then_inc(cur_ready, 1)

            def split_h(j, u, gg):
                n = (2 * u + gg) % NH
                hi, lo = (hsp[:, n, s, :, :].rearrange("p c n -> p (c n)") for s in range(2))
                s_h = cur[:, u % RING, C_H:C_H + 1]
                if gg == 0:
                    dve.wait_ge(cur_ready, j + 1)
                dve.wait_ge(h_hi, 2 * j + gg + 1)
                v.scalar_tensor_tensor(out=lo, in0=h32[:, gg, :], scalar=s_h, in1=hi,
                                       op0=ALU.mult, op1=ALU.subtract).then_inc(h_split, 1)

            def rows_out(j, u, e):
                r = u % RING
                s_o = cur[:, r, C_O:C_O + 1]
                dve.wait_ge(l2_done, j + 1)
                if not (isinstance(j, int) and j < RING):
                    dve.wait_ge(added, 16 * (j - RING + 1))
                v.scalar_tensor_tensor(out=outb[:, r, :], in0=ps[:, OB + r, 0:D], scalar=s_o,
                                       in1=b2bc[:, bass.ds(e, 1), :].rearrange("p a d -> p (a d)"),
                                       op0=ALU.mult, op1=ALU.add).then_inc(o_sum, 1)
                dve.wait_ge(o_sum, j + 1)
                v.scalar_tensor_tensor(out=outb[:, r, :], in0=ps[:, OB + r, D:2 * D], scalar=s_o, in1=outb[:, r, :],
                                       op0=ALU.mult, op1=ALU.add).then_inc(o_read, 1)

            def turn(j, u, first=False, turned=True, split=()):
                e_out = None if first else expert_of(ON_DVE, j - 1)
                e_in = expert_of(ON_DVE, j + 2) if turned else None
                split_h(j, u, 1)
                if turned:
                    split_x(j + 2, u + 2)
                for n in split[:1]:
                    split_lo(n)
                if not first:
                    if isinstance(j, int) and j == 1:
                        dve.wait_ge(b2_in, 16)
                    rows_out(j - 1, u - 1 + RING, e_out)
                split_h(j + 1, u + 1, 0)
                if turned:
                    expert_table(j + 2, u + 2, e_in)
                for n in split[1:]:
                    split_lo(n)
                    tables(n // 2, n // 2 + 1)

            dve.wait_ge(y_written, 16 * 4)
            for j in range(2):
                split_x(j, j)
                expert_table(j, j, j)
            for n in (4, 5):
                split_lo(n)
            split_h(0, 0, 0)
            dve.wait_ge(te_ready, 1)
            for j in range(PEELED * RING):
                turn(j, j % RING, first=(j == 0),
                     split=range(GAP + 2 * j, min(GAP + 2 * j + 2, 2 * E)))
            with dve.Fori(0, (LAST - PEELED) // BODY) as i:
                for u in range(BODY * RING):
                    turn(RING * (PEELED + BODY * i) + u, u % RING)
            turn(NT - 3, 0)
            turn(NT - 2, 1, turned=False)
            split_h(NT - 1, 2, 1)
            for j in (NT - 2, NT - 1):
                rows_out(j, j % RING, expert_of(ON_DVE, j))


_INS = ["x", "cond_1024", "L0_cond_weight", "L0_ffn_router_w", "L0_ffn_router_b", "L0_ffn_lang_w", "L0_ffn_lang_b",
        "L0_ffn_w1", "L0_ffn_b1", "L0_ffn_w2", "L0_ffn_b2"]


def kernel(**inputs):
    import numpy as _np
    import concourse.bacc as _bacc
    from concourse import mybir as _mybir
    from concourse.bass_utils import run_bass_kernel_spmd as _run

    nc = _bacc.Bacc("TRN2", target_bir_lowering=False, num_devices=1)
    arrays, args = {}, []
    for name in _INS:
        a = _np.ascontiguousarray(inputs[name])
        arrays[f"in_{name}"] = a
        args.append(nc.dram_tensor(f"in_{name}", a.shape, _mybir.dt.from_np(a.dtype), kind="ExternalInput").ap())
    args.append(nc.dram_tensor("out_0", (N + P, D), _mybir.dt.float32, kind="ExternalOutput").ap())
    adaln_moe(nc, *args)
    r = _run(nc, [arrays], core_ids=[0])
    return r.results[0]["out_0"][0:N].reshape(NB, SEQ, D)
```

```python
from contextlib import ExitStack

import concourse.bass as bass
from concourse import mybir

F32, F16 = mybir.dt.float32, mybir.dt.float16
I16, I32, U32 = mybir.dt.int16, mybir.dt.int32, mybir.dt.uint32
ALU, ACT, AX = mybir.AluOpType, mybir.ActivationFunctionType, mybir.AxisListType
ON_PE, ON_DVE = mybir.EngineType.PE, mybir.EngineType.DVE
RED = bass.bass_isa.ReduceOp

P = 128
NB, SEQ, D = 2, 1024, 256
E, L, F = 8, 4, 1024
NR = E + L
N = NB * SEQ
T = N // P
TB = T // NB
K = 2
NT = N * K // P + E - 1
KD, KF = D // P, F // P
GH = KF // 2
ROW = D + E
EPS = 1e-8
HALF = KD * F
SLOTS = 4
RING = 3
ROWS = 5
LAST = NT // RING - 1
HI_ACT = range(6, 7)
EARLY = 2
GAP = 6
PEELED = 2
BODY = 5
RANKS_AT = 8
WARM = 18
KEEP = 1
XB3 = 3
YB = (4, 5, 6, 1)
NH = 2 * RING
BIG = 1e30

FIELD_SCALE = 268 - 64
FIELD_GELU = 27
FIELD_MAX = 254
ULP = float(1 << 23)
ROUND = 1.5 * ULP
FIELD_H = 389 - 128
FIELD_HB = 267
FIELD_O = 113 + 64

C_GELU, C_H, C_O, C_P, NCUR = KF, KF + 1, KF + 2, KF + 3, KF + 4


def adaln_moe(nc, x, cond, cw, rw, rb, lw, lb, w1, b1, w2, b2, out):
    y_rows = nc.dram_tensor("y_rows", (N + P, ROW), F32, kind="Internal").ap()
    x_tiles = x.rearrange("b (t p) d -> p (b t) d", p=P)
    w1_v = w1.rearrange("e (k p) f -> e p k f", p=P)
    w2_v = w2.rearrange("e (c p) d -> e p c d", p=P)

    ctx = ExitStack()
    with ctx:
        def sb(name, shape, dt=F32):
            return ctx.enter_context(nc.sbuf_tensor(name, shape, dt))

        def sem(name):
            return ctx.enter_context(nc.semaphore(name))

        wsp = sb("wsp", [P, E, 4 * HALF], F16)
        stage = sb("stage", [P, SLOTS, HALF])
        pay = sb("pay", [P, T * ROW])
        onehot = sb("onehot", [P, K * T * P], F16)
        b2bc = sb("b2bc", [P, E, D])
        tilehot = sb("tilehot", [P, NT, K * T], F16)
        rows = sb("rows", [P, ROWS, ROW])
        scratch = wsp[:, E - 2, :].bitcast(F32)
        xin_flat = wsp[:, E - 1, :].bitcast(F32)
        xin = xin_flat.rearrange("p (t d) -> p t d", t=T)
        at = [0]

        def carve(n):
            at[0] += n
            assert at[0] <= 2 * HALF
            return scratch[:, at[0] - n:at[0]]

        W = carve(KD * D).rearrange("p (k d) -> p k d", k=KD)
        WT = carve(KD * D).rearrange("p (o i) -> p o i", o=KD)
        Wsq = carve(KD * D).rearrange("p (k d) -> p k d", k=KD)
        squares = scratch[:, KD * D:3 * KD * D].rearrange("p (t d) -> p t d", t=4)
        Wy = carve(NB * KD * D).rearrange("p (b k n) -> p b k n", b=NB, k=KD)
        Wr = carve(NB * KD * NR).rearrange("p (b k n) -> p b k n", b=NB, k=KD)
        xT = pay[:, :].rearrange("p (t r) -> p t r", t=T)[:, :, 0:D]
        ident = sb("ident", [P, P])
        tri = sb("tri", [P, P], F16)
        ones = sb("ones", [P, P], F16)
        iota = wsp[:, 4, 0:P * K * T].bitcast(I16).rearrange("p (s c) -> p s c", c=K * T)
        first = sb("first", [P, E], I32)
        home = sb("home", [P, E], I32)
        tok1 = sb("tok1", [P, K * T], I32)
        tok16 = sb("tok16", [P, K * T], F16)
        padi = sb("padi", [P, 1], I32)
        padf = sb("padf", [P, 1])
        te = sb("te", [1, NT], I32)
        condr = sb("condr", [NB * KD, P])
        ys = sb("ys", [P, KD, NB])
        ysq = sb("ysq", [P, KD, NB])
        RL = sb("RL", [NR, D])
        biasr = sb("biasr", [P, NR])
        R = sb("R", [P, KD, NR])
        Rd = sb("Rd", [P, KD, NB, NR])
        dv = sb("dv", [P, 5, KD * NB])
        dcol = sb("dcol", [P, KD, NB])
        b1r = sb("b1r", [E * KF, P])
        tab = sb("tab", [P, E, NCUR])
        cur = sb("cur", [P, RING, NCUR])
        wsum = sb("wsum", [P, 2 * E])
        wmax = sb("wmax", [P, 2 * E])
        wround = sb("wround", [P, 2 * E])
        wt = sb("wt", [P, 2 * E])
        wscale = sb("wscale", [P, 2 * E])
        ysum = sb("ysum", [P, T // 4])
        ysm = sb("ysm", [P, 1])
        ymax = sb("ymax", [P, 1])
        yt = sb("yt", [P, 1], I32)
        yscale = sb("yscale", [P, 1])
        bmx = sb("bmx", [P, E])
        bmax = sb("bmax", [P, E])
        bfield = sb("bfield", [P, E], I32)
        fld = sb("fld", [P, 2, E])
        nfb = sb("nfb", [P, E])
        yg = sb("yg", [P, 2])
        s1 = sb("s1", [P, 8, T])
        M16 = sb("M16", [P, T, E], F16)
        Mt = sb("Mt", [P, E], F16)
        tl = sb("tl", [P, 4, L + E])
        base = sb("base", [P, 3, E])
        tli = sb("tli", [P, 2, E], I32)
        tef = sb("tef", [1, NT - E])
        slot = sb("slot", [P, 3, K * T], I16)
        idx = sb("idx", [P, NT], U32)
        warm = sb("warm", [P, 1])

        route_at = [0]

        def share(*shape):
            n = 1
            for q in shape:
                n *= q
            route_at[0] += n
            assert route_at[0] <= E * D
            flat = b2bc[:, :, :].rearrange("p e d -> p (e d)")[:, route_at[0] - n:route_at[0]]
            return flat.rearrange("p (t e) -> p t e", t=shape[0]) if len(shape) == 2 else flat.rearrange(
                "p (k t e) -> p k t e", k=shape[0], t=shape[1])

        lg, lpp, le = share(T, NR), share(T, L + 1), share(T, L)
        cmp, tiles_i = share(NT - E, E)[0:1], share(NT - E, E)[0:1].bitcast(I32)
        padv = share(1, NT)[:, 0, :]
        eq, r2, oh = share(T, E), share(T, E), share(K, T, E)
        own = share(K, T, E)

        payv = pay[:, :].rearrange("p (t r) -> p t r", t=T)
        h32 = pay[:, 0:2 * GH * P].rearrange("p (g n) -> p g n", g=2)
        hsp = pay[:, 2 * GH * P:2 * GH * P + NH * GH * P].bitcast(F16).rearrange(
            "p (h s c n) -> p h s c n", h=NH, s=2, c=GH)
        ohv = onehot[:, :].rearrange("p (s c) -> p s c", s=P)
        xsp = onehot[:, 0:RING * 2 * D].rearrange("p (r s k n) -> p r s k n", r=RING, s=2, k=KD)
        outb = onehot[:, RING * 2 * D:RING * 4 * D].bitcast(F32).rearrange("p (r n) -> p r n", r=RING)

        ps = ctx.enter_context(nc.psum_tensor("ps", [P, 8, 512], F32))
        HB, OB, XB, MB = 0, 3, 6, 7

        consts = sem("consts"); iota_ready = sem("iota_ready"); small_in = sem("small_in"); cond_in = sem("cond_in")
        cw_in = sem("cw_in"); x_in = [sem(f"x_in{c}") for c in range(4)]
        w_in = [sem(f"w_in{i}") for i in range(SLOTS + 2)]
        b2_in = sem("b2_in"); pads_out = sem("pads_out"); x_copied = sem("x_copied"); y_written = sem("y_written")
        zero_ready = sem("zero_ready")
        cond_psum = sem("cond_psum"); wr_ready = sem("wr_ready"); lg_psum = sem("lg_psum"); lg_read = sem("lg_read")
        warm_ready = sem("warm_ready"); pool_step = sem("pool_step"); cur_ready = sem("cur_ready")
        wt_psum = sem("wt_psum"); wt_ready = sem("wt_ready"); rb_psum = sem("rb_psum")
        sq_ready = sem("sq_ready"); v_psum = sem("v_psum"); v_ready = sem("v_ready"); v_root = sem("v_root")
        d_ready = sem("d_ready"); rd_ready = sem("rd_ready"); d_psum = sem("d_psum"); wr_psum = sem("wr_psum")
        wp_ready = sem("wp_ready"); b1_ready = sem("b1_ready"); b1_max = sem("b1_max")
        xt_psum = sem("xt_psum"); xt_ready = sem("xt_ready"); y_psum = sem("y_psum"); y_ready = sem("y_ready")
        y_sq = sem("y_sq"); ym_ready = sem("ym_ready"); y_max = sem("y_max")
        lang_in = sem("lang_in"); lang_exp = sem("lang_exp"); gap_in = sem("gap_in"); gap_exp = sem("gap_exp")
        picked = sem("picked"); p_ready = sem("p_ready"); counted = sem("counted"); ranked = sem("ranked")
        tile_hot = sem("tile_hot"); hot_ready = sem("hot_ready")
        mapped = sem("mapped"); idx_ready = sem("idx_ready"); te_ready = sem("te_ready")
        w_sq = sem("w_sq"); w_scaled = sem("w_scaled"); w_t = sem("w_t"); w_hi_pool = sem("w_hi_pool")
        w_hi_act = sem("w_hi_act"); w_split = sem("w_split")
        tab_ready = sem("tab_ready"); field_h = sem("field_h"); field_o = sem("field_o")
        dve_step = sem("dve_step")
        gathered = [sem(f"gathered{r}") for r in range(ROWS)]
        t_done = sem("t_done"); ys_ready = sem("ys_ready"); x_hi = sem("x_hi"); x_split = sem("x_split")
        l1_done = sem("l1_done"); gelu_done = sem("gelu_done"); h_hi_act = sem("h_hi_act")
        h_hi_dve = sem("h_hi_dve"); h_split = sem("h_split")
        l2_done = sem("l2_done"); o_sum = sem("o_sum"); o_read = sem("o_read"); o_ready = sem("o_ready")
        added = sem("added")

        def parts_of(n):
            e = n // 2
            if n % 2 == 0:
                return [wsp[:, e, s * HALF:(s + 1) * HALF].rearrange("p (c d) -> p c d", d=D) for s in range(2)]
            both = wsp[:, e, 2 * HALF:4 * HALF].rearrange("p (c s d) -> p c s d", c=KF, s=2)
            return [both[:, :, s, :] for s in range(2)]

        def wait_hi(eng, n):
            if n in HI_ACT:
                eng.wait_ge(w_hi_act, n - HI_ACT[0] + 1)
            else:
                eng.wait_ge(w_hi_pool, n + 1 - (len(HI_ACT) if n > HI_ACT[0] else 0))

        def wait_split(eng, n):
            eng.wait_ge(w_split, n + 1)

        def place(n):
            return n % SLOTS if n < 6 else n - 6 + SLOTS if n < 8 else (n - 6) % SLOTS

        def earlier(n):
            return [m for m in range(n) if place(m) == place(n)]

        def staged(n):
            flat = stage[:, place(n), :] if place(n) < SLOTS else xin_flat[:, (place(n) - SLOTS) * HALF:][:, 0:HALF]
            return flat.rearrange("p (c d) -> p c d", d=D)

        def experts_of(engine, j, n):
            _, values = nc.values_load_multi_w_load_instructions(
                te[0:1, bass.ds(j, n)], engines=(engine,), min_val=0, max_val=E - 1,
                skip_runtime_bounds_check_because="te counts experts and is cut off at the last one")
            return values

        def expert_of(engine, j):
            return j if isinstance(j, int) and j < E else experts_of(engine, j, 1)[0]

        block = ctx.enter_context(nc.Block())

        @block.sync
        def _(sp):
            sp.dma_start(condr[:, :], cond.rearrange("b (k p) -> (b k) p", p=P)).then_inc(cond_in, 16)
            sp.dma_start(W, cw.rearrange("(k p) d -> p k d", p=P)).then_inc(cw_in, 16)

            def load_x(c):
                sp.dma_start(xin[:, 4 * c:4 * c + 4, :], x_tiles[:, 4 * c:4 * c + 4, :]).then_inc(x_in[c], 16)

            load_x(0)
            sp.dma_start(RL[0:E, :], rw).then_inc(small_in, 16)
            sp.dma_start(RL[E:NR, :], lw).then_inc(small_in, 16)
            sp.dma_start(b1r[:, :], b1.rearrange("e (c p) -> (e c) p", p=P)).then_inc(small_in, 16)
            sp.dma_start(biasr[:, 0:E], rb.rearrange("(a n) -> a n", a=1).broadcast_to([P, E])).then_inc(small_in, 16)
            sp.dma_start(biasr[:, E:NR], lb.rearrange("(a n) -> a n", a=1).broadcast_to([P, L])).then_inc(small_in, 16)

            def load_weights(n):
                if earlier(n):
                    wait_split(sp, earlier(n)[-1])
                if n == 6:
                    sp.wait_ge(xt_psum, T // 2)
                src = (w1_v if n % 2 == 0 else w2_v)[n // 2]
                dst = staged(n).rearrange("p (k a) d -> p k (a d)", k=KD if n % 2 == 0 else KF)
                sp.dma_start(dst, src).then_inc(w_in[place(n)], 16)

            load_weights(0)
            load_x(1)
            load_weights(1)
            load_x(2)
            load_x(3)
            for n in range(2, SLOTS):
                load_weights(n)
            sp.wait_ge(zero_ready, 1)
            sp.dma_start(y_rows[N:N + P, :], rows[:, 0, :]).then_inc(pads_out, 16)
            sp.dma_start(out[N:N + P, :], rows[:, 0, 0:D]).then_inc(pads_out, 16)
            for n in range(SLOTS, 8):
                load_weights(n)

            def copy_x(b):
                sp.dma_start(out[b * SEQ:(b + 1) * SEQ, :], x[b]).then_inc(x_copied, 16)

            copy_x(0)
            sp.wait_ge(p_ready, 1)
            for c in range(4):
                sp.wait_ge(y_ready, 4 * c + 4)
                sp.dma_start(y_rows[0:N, :].rearrange("(t p) r -> p t r", p=P)[:, 4 * c:4 * c + 4, :],
                             payv[:, 4 * c:4 * c + 4, :]).then_inc(y_written, 16)
            copy_x(1)
            for j in range(RING):
                sp.wait_ge(gathered[j], 16)
            for n in range(8, 10):
                load_weights(n)
            sp.wait_ge(idx_ready, 1)
            sp.dma_start(b2bc[:, :, :].rearrange("p e d -> p (e d)"),
                         b2.rearrange("(a e) d -> a (e d)", a=1).broadcast_to([P, E * D])).then_inc(b2_in, 16)
            for n in range(10, 2 * E):
                load_weights(n)

        @block.gpsimd
        def _(pool):
            g = nc.gpsimd
            g.memset(warm[:, :], 0.0).then_inc(warm_ready, 1)
            g.memset(ident[:, :], 0.0).then_inc(consts, 1)
            g.memset(tri[:, :], 1.0).then_inc(consts, 1)
            g.memset(ones[:, :], 1.0).then_inc(consts, 1)
            g.iota(first[:, :], pattern=[[-1, E]], base=E, channel_multiplier=0).then_inc(consts, 1)
            g.iota(home[:, :], pattern=[[P, E]], base=0, channel_multiplier=0).then_inc(consts, 1)
            g.iota(tok1[:, :], pattern=[[0, K], [P, T]], base=1, channel_multiplier=1).then_inc(consts, 1)
            g.iota(padi[:, :], pattern=[[0, 1]], base=N + 1, channel_multiplier=1).then_inc(consts, 1)
            g.iota(tiles_i[:, :, :], pattern=[[1, NT - E], [0, E]], base=0, channel_multiplier=0).then_inc(consts, 1)
            g.iota(te[:, 0:E], pattern=[[1, E]], base=0, channel_multiplier=0).then_inc(consts, 1)
            g.memset(lpp[:, :, L:L + 1], 0.0).then_inc(consts, 1)
            g.memset(tl[:, :, 0:L], 0.0).then_inc(consts, 1)
            g.memset(rows[:, 0, :], 0.0).then_inc(zero_ready, 1)
            pool.wait_ge(consts, 11)
            g.affine_select(out=ident[:, :], in_=ident[:, :], compare_op=ALU.not_equal, fill=1.0, base=0,
                            pattern=[[-1, P]], channel_multiplier=1).then_inc(consts, 1)
            g.affine_select(out=tri[:, :], in_=tri[:, :], compare_op=ALU.is_gt, fill=0.0, base=0,
                            pattern=[[1, P]], channel_multiplier=-1).then_inc(consts, 1)
            g.tensor_copy(padf[:, :], padi[:, :]).then_inc(consts, 1)
            g.tensor_copy(tok16[:, :], tok1[:, :]).then_inc(consts, 1)

            g.iota(iota[:, :, :], pattern=[[1, P], [0, K * T]], base=0, channel_multiplier=0).then_inc(iota_ready, 1)
            psteps = [0]

            def step(ins):
                psteps[0] += 1
                ins.then_inc(pool_step, 1)
                pool.wait_ge(pool_step, psteps[0])

            def scale_weights(n):
                pool.wait_ge(w_sq, n + 1)
                step(g.partition_all_reduce(wmax[:, n:n + 1], wsum[:, n:n + 1], P, RED.max))
                step(g.tensor_scalar(wround[:, n:n + 1], wmax[:, n:n + 1].bitcast(I32), 2.0 ** -24, ROUND,
                                     ALU.mult, ALU.add))
                g.tensor_scalar(wscale[:, n:n + 1].bitcast(I32), wround[:, n:n + 1], -ULP,
                                (FIELD_SCALE + 1 + ROUND) * ULP, ALU.mult, ALU.add).then_inc(w_scaled, 1)
                g.tensor_scalar(wt[:, n:n + 1], wround[:, n:n + 1], -(ROUND + 1), 1.0, ALU.add, ALU.mult).then_inc(w_t, 1)

            def split_hi(n):
                if n // 2 == E - 2:
                    pool.wait_ge(y_psum, T)
                if n // 2 == E - 1:
                    wait_split(pool, 7)
                pool.wait_ge(w_scaled, n + 1)
                g.tensor_scalar(parts_of(n)[0], staged(n), wscale[:, n:n + 1], 1.0,
                                ALU.mult, ALU.mult).then_inc(w_hi_pool, 1)

            pool.wait_ge(b1_ready, 1)
            g.partition_all_reduce(bmax[:, :], bmx[:, :], P, RED.max).then_inc(b1_max, 1)
            for n in range(HI_ACT[0] - 1):
                scale_weights(n)
                split_hi(n)

            def gather(j):
                g.indirect_dma_start(out=rows[:, j % ROWS, :], out_offset=None, in_=y_rows,
                                     in_offset=bass.IndirectOffsetOnAxis(ap=idx[:, j:j + 1], axis=0)
                                     ).then_inc(gathered[j % ROWS], 16)

            pool.wait_ge(ym_ready, 1)
            g.partition_all_reduce(ymax[:, :], ysm[:, :], P, RED.max).then_inc(y_max, 1)
            scale_weights(5)
            pool.wait_ge(y_written, 16 * 4)
            pool.wait_ge(pads_out, 32)
            pool.wait_ge(idx_ready, 1)
            for j in range(RING):
                gather(j)
            split_hi(5)
            scale_weights(6)
            for j in range(RING, ROWS):
                gather(j)
            for j in range(NT):
                if j + ROWS < NT:
                    pool.wait_ge(cur_ready, j + 1)
                    gather(j + ROWS)
                for n in range(GAP + (2 * j + 3 if j else 1), min(GAP + 2 * j + 5, 2 * E)):
                    scale_weights(n)
                    split_hi(n)
                if j == 0:
                    pool.wait_ge(x_copied, 16 * NB)
                pool.wait_ge(o_ready, j + 1)
                if j:
                    pool.wait_ge(added, 16 * j)
                g.indirect_dma_start(out=out, out_offset=bass.IndirectOffsetOnAxis(ap=idx[:, j:j + 1], axis=0),
                                     in_=outb[:, j % RING, :], in_offset=None,
                                     compute_op=ALU.add).then_inc(added, 16)
            pool.wait_ge(added, 16 * NT)

        @block.tensor
        def _(pe):
            mm, tr = nc.tensor.matmul, nc.tensor.transpose
            pe.wait_ge(consts, 15)
            pe.wait_ge(cond_in, 16)
            tr(ps[:, 7, 0:NB * KD], condr[:, :], ident[0:NB * KD, 0:NB * KD]).then_inc(cond_psum, 1)
            pe.wait_ge(cw_in, 16)
            for o in range(KD):
                for k in range(KD):
                    last = tr(ps[:, 0, (o * KD + k) * P:(o * KD + k + 1) * P], W[:, k, o * P:(o + 1) * P], ident[:, :])
            last.then_inc(wt_psum, 1)
            pe.wait_ge(sq_ready, 1)
            for o in range(KD):
                for k in range(KD):
                    last = mm(ps[:, 2, o * NB:(o + 1) * NB], Wsq[:, k, o * P:(o + 1) * P], ysq[:, k, :],
                              start=(k == 0), stop=(k == KD - 1))
            last.then_inc(v_psum, 1)
            pe.wait_ge(small_in, 16 * 5)
            for k in range(KD):
                tr(ps[:, 1, k * NR:(k + 1) * NR], RL[:, k * P:(k + 1) * P], ident[0:NR, 0:NR])
            tr(ps[:, 1, 64:64 + E * KF], b1r[:, :], ident[0:E * KF, 0:E * KF]).then_inc(rb_psum, 1)

            def transpose_x(q):
                if q % 2 == 0:
                    pe.wait_ge(x_in[q // 2], 16)
                if q >= XB3:
                    pe.wait_ge(xt_ready, q - XB3 + 1)
                for t in range(2):
                    for k in range(KD):
                        last = tr(ps[:, 5 + q % XB3, (t * KD + k) * P:(t * KD + k + 1) * P],
                                  xin[:, 2 * q + t, k * P:(k + 1) * P], ident[:, :])
                last.then_inc(xt_psum, 1)

            transpose_x(0)
            pe.wait_ge(rd_ready, 1)
            pe.wait_ge(wt_ready, 1)
            for k in range(KD):
                for o in range(KD):
                    last = mm(ps[:, 4, k * NB * NR:(k + 1) * NB * NR], WT[:, o, k * P:(k + 1) * P],
                              Rd[:, o, :, :].rearrange("p b n -> p (b n)"), start=(o == 0), stop=(o == KD - 1))
            last.then_inc(wr_psum, 1)
            for b in range(NB):
                for o in range(KD):
                    last = mm(ps[:, 3, b * D + o * P:b * D + (o + 1) * P],
                              dcol[:, o, b:b + 1].broadcast_to([P, P]), ident[:, :], start=True, stop=True)
            last.then_inc(d_psum, 1)
            transpose_x(1)
            pe.wait_ge(wr_ready, 1)
            for q in range(T // 2):
                if q + 2 < T // 2:
                    transpose_x(q + 2)
                pe.wait_ge(xt_ready, q + 1)
                for _ in range(KEEP):
                    mm(ps[:, 2, 256:512], ones[:, :], ones[:, 0:1].broadcast_to([P, 256]), start=True, stop=True)
                for t in (2 * q, 2 * q + 1):
                    for k in range(KD):
                        last = mm(ps[:, 0, t * NR:(t + 1) * NR], xT[:, t, k * P:(k + 1) * P], Wr[:, t // TB, k, :],
                                  start=(k == 0), stop=(k == KD - 1))
            last.then_inc(lg_psum, 1)

            def rows_of_y(t):
                if t >= 4:
                    pe.wait_ge(y_ready, t - 3)
                for k in range(KD):
                    last = mm(ps[:, YB[t % 4], 0:D], xT[:, t, k * P:(k + 1) * P], Wy[:, t // TB, k, :],
                              start=(k == 0), stop=(k == KD - 1))
                last.then_inc(y_psum, 1)

            pe.wait_ge(wp_ready, 1)
            pe.wait_ge(xt_ready, T // 2)
            for t in range(RANKS_AT):
                rows_of_y(t)
            pe.wait_ge(picked, 1)
            mm(ps[:, 3, 0:E], ones[:, :], Mt[:, :], start=True, stop=True).then_inc(counted, 1)
            mm(ps[:, 2, 0:T * E], tri[:, :], M16[:, :, :].rearrange("p t e -> p (t e)"), start=True, stop=False)
            for t in range(T - 1):
                last = mm(ps[:, 2, (t + 1) * E:T * E].rearrange("p (a e) -> p a e", e=E), ones[:, :],
                          M16[:, t:t + 1, :].broadcast_to([P, T - 1 - t, E]), start=False, stop=(t == T - 2))
            last.then_inc(ranked, 1)
            for t in range(RANKS_AT, T):
                rows_of_y(t)
            pe.wait_ge(hot_ready, 1)
            for c in range(K * T):
                last = mm(ps[:, MB, 0:NT], ohv[:, :, c], tilehot[:, :, c], start=(c == 0), stop=(c == K * T - 1))
            last.then_inc(mapped, 1)
            for _ in range(WARM):
                mm(ps[:, 0, :], ones[:, :], onehot[:, 0:512], start=True, stop=True)
            pe.wait_ge(y_ready, T)


            def transpose_rows(j, s, i=0):
                pe.wait_ge(gathered[s % ROWS], 16 * (s // ROWS + 1 + BODY * RING // ROWS * i))
                if not (isinstance(j, int) and j == 0):
                    pe.wait_ge(x_split, j)
                for k in range(KD):
                    last = tr(ps[:, XB, k * P:(k + 1) * P], rows[:, s % ROWS, k * P:(k + 1) * P], ident[:, :])
                last.then_inc(t_done, 1)

            def blocks(uj, us, ue, gg, dj, ds, de, dg, turned=True):
                if uj is not None:
                    if isinstance(uj, int) and uj < E:
                        wait_split(pe, 2 * uj)
                    if gg == 0 and (dj is None or not turned):
                        pe.wait_ge(x_split, uj + 1)
                if dj is not None:
                    if isinstance(dj, int) and dj < E:
                        wait_split(pe, 2 * dj + 1)
                    pe.wait_ge(h_split, 2 * dj + dg + 1)
                up_last = down_last = None
                for c in range(GH):
                    if uj is not None:
                        steps = [(0, 0, 0), (0, 0, 1), (0, 1, 0), (0, 1, 1), (1, 0, 0), (1, 1, 0)]
                        for q, (w, k, part) in enumerate(steps):
                            o = w * HALF + k * F + (gg * GH + c) * P
                            up_last = mm(ps[:, HB + (2 * us + gg) % RING, c * P:(c + 1) * P],
                                         wsp[:, bass.ds(ue, 1), o:o + P].rearrange("p a f -> p (a f)"),
                                         xsp[:, us % RING, part, k, :], start=(q == 0), stop=(q == len(steps) - 1))
                    if dj is not None:
                        cc = dg * GH + c
                        for part, width in ((0, 2 * D), (1, D)):
                            o = 2 * HALF + cc * 2 * D
                            down_last = mm(ps[:, OB + ds % RING, 0:width], hsp[:, (2 * ds + dg) % NH, part, c, :],
                                           wsp[:, bass.ds(de, 1), o:o + width].rearrange("p a f -> p (a f)"),
                                           start=(cc == 0 and part == 0), stop=(cc == KF - 1 and part == 1))
                if uj is not None:
                    up_last.then_inc(l1_done, 1)
                if dj is not None and dg == 1:
                    down_last.then_inc(l2_done, 1)

            def turn(j, s, e_before, e_now, e_next, i=0, first=False, turned=True):
                if turned:
                    transpose_rows(j + 2, s + 2, i)
                down = (None, 0, 0, 0) if first else (j - 1, s - 1, e_before, 1)
                blocks(j + 1, s + 1, e_next, 0, *down, turned=turned)
                blocks(j + 1, s + 1, e_next, 1, j, s, e_now, 0)

            transpose_rows(0, 0)
            transpose_rows(1, 1)
            for gg in range(2):
                blocks(0, 0, 0, gg, None, 0, 0, 0)
            for j in range(PEELED * RING):
                turn(j, j, j - 1, j, j + 1, first=(j == 0))
            pe.wait_ge(te_ready, 1)
            wait_split(pe, 2 * E - 1)
            with pe.Fori(0, (LAST - PEELED) // BODY) as i:
                start = RING * PEELED + RING * BODY * i
                e = experts_of(ON_PE, start - 1, 2)
                for u in range(BODY * RING):
                    if u % RING == 0:
                        e = e[-2:] + experts_of(ON_PE, start + u + 1, RING)
                    turn(start + u, RING * PEELED + u, *e[u % RING:u % RING + 3], i=i)
            j = RING * LAST
            es = experts_of(ON_PE, j - 1, RING + 1)
            turn(j, j, es[0], es[1], es[2])
            turn(j + 1, j + 1, es[1], es[2], es[3], turned=False)
            blocks(None, 0, 0, 0, j + 1, j + 1, es[2], 1)
            for dg in range(2):
                blocks(None, 0, 0, 0, j + 2, j + 2, es[3], dg)

        @block.scalar
        def _(act):
            a = nc.scalar
            act.wait_ge(warm_ready, 1)
            a.activation(warm[:, :], warm[:, :], ACT.Sqrt)
            act.wait_ge(wt_psum, 1)
            a.activation(WT.rearrange("p o i -> p (o i)"), ps[:, 0, :], ACT.Copy).then_inc(wt_ready, 1)
            act.wait_ge(v_ready, 1)
            a.activation(dv[:, 1, :], dv[:, 0, :], ACT.Sqrt).then_inc(v_root, 1)
            a.activation(ymax[:, :], dv[:, 0, 0:1], ACT.Exp).then_inc(warm_ready, 1)

            def square_weights(n):
                act.wait_ge(w_in[place(n)], 16 * (len(earlier(n)) + 1))
                if n // 2 == E - 2:
                    act.wait_ge(y_psum, T)
                if n // 2 == E - 1:
                    wait_split(act, 7)
                a.activation(parts_of(n)[1], staged(n), ACT.Square, accum_out=wsum[:, n:n + 1]).then_inc(w_sq, 1)

            def split_hi(n):
                act.wait_ge(w_scaled, n + 1)
                a.activation(parts_of(n)[0], staged(n), ACT.Copy, scale=wscale[:, n:n + 1]).then_inc(w_hi_act, 1)

            square_weights(0)
            for q in range(T // 2):
                act.wait_ge(xt_psum, q + 1)
                a.activation(xT[:, 2 * q:2 * q + 2, :], ps[:, 5 + q % XB3, :].rearrange("p (t n) -> p t n", t=2),
                             ACT.Copy).then_inc(xt_ready, 1)
                if q == 1:
                    square_weights(1)
            square_weights(2)
            act.wait_ge(lang_in, 1)
            a.activation(le[:, :, :], lpp[:, :, 0:L], ACT.Exp).then_inc(lang_exp, 1)
            for t in range(T):
                act.wait_ge(y_psum, t + 1)
                a.activation(payv[:, t, 0:D], ps[:, YB[t % 4], 0:D], ACT.Copy).then_inc(y_ready, 1)
                if t % 4 == 3:
                    c = t // 4
                    act.wait_ge(y_ready, t + 1)
                    a.activation(squares, payv[:, 4 * c:4 * c + 4, 0:D], ACT.Square,
                                 accum_out=ysum[:, c:c + 1]).then_inc(y_sq, 1)
                if t == 1:
                    square_weights(3)
                if t == 5:
                    act.wait_ge(gap_in, 1)
                    a.activation(s1[:, 5, :], s1[:, 4, :], ACT.Exp).then_inc(gap_exp, 1)
                    square_weights(4)
            square_weights(5)
            square_weights(6)
            a.activation(warm[:, :], s1[:, 4, 0:1], ACT.Gelu)

            def x_high(j, s):
                act.wait_ge(t_done, j + 1)
                a.activation(xsp[:, s % RING, 0, :, :].rearrange("p k n -> p (k n)"), ps[:, XB, 0:D], ACT.Copy,
                             scale=yscale[:, 0:1]).then_inc(x_hi, 1)

            def gelus(j, s, gg):
                n = 2 * (s % RING) + gg
                if gg == 0:
                    act.wait_ge(cur_ready, j + 1)
                act.wait_ge(l1_done, 2 * j + gg + 1)
                if not (isinstance(j, int) and j == 0):
                    act.wait_ge(h_split, 2 * j + gg - 1)
                for c in range(GH):
                    cc = gg * GH + c
                    last = a.activation(h32[:, gg, c * P:(c + 1) * P], ps[:, HB + n % RING, c * P:(c + 1) * P],
                                        ACT.Gelu, bias=cur[:, s % RING, cc:cc + 1],
                                        scale=cur[:, s % RING, C_GELU:C_GELU + 1])
                last.then_inc(gelu_done, 1)
                if gg == 1:
                    return
                act.wait_ge(gelu_done, 2 * j + 1)
                a.activation(hsp[:, n, 0, :, :].rearrange("p c n -> p (c n)"), h32[:, gg, :], ACT.Copy,
                             scale=cur[:, s % RING, C_H:C_H + 1]).then_inc(h_hi_act, 1)

            def weigh(j, s):
                r = s % RING
                act.wait_ge(o_read, j + 1)
                a.activation(outb[:, r, :], outb[:, r, :], ACT.Copy, scale=cur[:, r, C_P:NCUR]).then_inc(o_ready, 1)

            def turn(j, s, first=False, turned=True, squares=()):
                gelus(j, s, 1)
                if turned:
                    x_high(j + 2, s + 2)
                for n in squares[:1]:
                    square_weights(n)
                gelus(j + 1, s + 1, 0)
                for n in squares[1:]:
                    square_weights(n)
                if not first:
                    weigh(j - 1, s - 1)

            act.wait_ge(ys_ready, 1)
            x_high(0, 0)
            x_high(1, 1)
            square_weights(7)
            gelus(0, 0, 0)
            split_hi(6)
            for j in range(PEELED * RING):
                turn(j, j, first=(j == 0), squares=range(GAP + 2 * j + 2, min(GAP + 2 * j + 4, 2 * E)))
            with act.Fori(0, (LAST - PEELED) // BODY) as i:
                for u in range(BODY * RING):
                    turn(RING * PEELED + RING * BODY * i + u, RING * PEELED + u)
            turn(NT - 3, NT - 3)
            turn(NT - 2, NT - 2, turned=False)
            gelus(NT - 1, NT - 1, 1)
            for j in (NT - 2, NT - 1):
                weigh(j, j)

        @block.vector
        def _(dve):
            v = nc.vector
            steps = [0]

            def step(ins):
                steps[0] += 1
                ins.then_inc(dve_step, 1)
                dve.wait_ge(dve_step, steps[0])

            def beside(ins):
                steps[0] += 1
                ins.then_inc(dve_step, 1)

            dve.wait_ge(cw_in, 16)
            v.tensor_tensor(Wsq, W, W, ALU.mult)
            dve.wait_ge(cond_psum, 1)
            step(v.tensor_scalar(ys[:, :, :], ps[:, 7, 0:NB * KD].rearrange("p (b k) -> p k b", b=NB), D ** -0.5, None,
                                 ALU.mult))
            v.tensor_tensor(ysq[:, :, :], ys[:, :, :], ys[:, :, :], ALU.mult).then_inc(sq_ready, 1)
            dve.wait_ge(v_psum, 1)
            v.tensor_scalar(dv[:, 0, :], ps[:, 2, 0:KD * NB], EPS, None, ALU.add).then_inc(v_ready, 1)
            dve.wait_ge(rb_psum, 1)
            step(v.tensor_copy(R[:, :, :], ps[:, 1, 0:KD * NR].rearrange("p (k n) -> p k n", k=KD)))
            step(v.tensor_copy(tab[:, :, 0:KF], ps[:, 1, 64:64 + E * KF].rearrange("p (e c) -> p e c", e=E)))
            v.tensor_reduce(bmx[:, :], tab[:, :, 0:KF], AX.X, ALU.max, apply_absolute_value=True).then_inc(b1_ready, 1)
            dve.wait_ge(v_root, 1)
            step(v.reciprocal(dv[:, 2, :], dv[:, 1, :]))
            step(v.tensor_tensor(dv[:, 3, :], dv[:, 2, :], dv[:, 2, :], ALU.mult))
            step(v.tensor_tensor(dv[:, 4, :], dv[:, 3, :], dv[:, 0, :], ALU.mult))
            step(v.tensor_scalar(dv[:, 3, :], dv[:, 4, :], -0.5, 1.5, ALU.mult, ALU.add))
            dve.wait_ge(v_ready, 1)
            v.tensor_tensor(dcol[:, :, :].rearrange("p o b -> p (o b)"), dv[:, 2, :], dv[:, 3, :],
                            ALU.mult).then_inc(d_ready, 1)
            dve.wait_ge(d_ready, 1)
            for b in range(NB):
                last = v.tensor_tensor(Rd[:, :, b, :], R[:, :, :], dcol[:, :, b:b + 1].broadcast_to([P, KD, NR]), ALU.mult)
            last.then_inc(rd_ready, 1)
            dve.wait_ge(wr_psum, 1)
            wr = ps[:, 4, 0:KD * NB * NR].rearrange("p (k b n) -> p b k n", k=KD, b=NB)
            for b in range(NB):
                last = v.tensor_tensor(Wr[:, b, :, :], wr[:, b, :, :], ys[:, :, b:b + 1].broadcast_to([P, KD, NR]), ALU.mult)
            last.then_inc(wr_ready, 1)
            dve.wait_ge(d_psum, 1)
            for b in range(NB):
                for k in range(KD):
                    last = v.scalar_tensor_tensor(out=Wy[:, b, k, :], in0=W[:, k, :], scalar=ys[:, k, b:b + 1],
                                                  in1=ps[:, 3, b * D:(b + 1) * D], op0=ALU.mult, op1=ALU.mult)
            last.then_inc(wp_ready, 1)

            def split_lo(n):
                hi, lo = parts_of(n)
                wait_hi(dve, n)
                v.scalar_tensor_tensor(out=lo, in0=staged(n), scalar=wscale[:, n:n + 1], in1=hi,
                                       op0=ALU.mult, op1=ALU.subtract).then_inc(w_split, 1)

            for n in range(EARLY):
                split_lo(n)
            dve.wait_ge(lg_psum, 1)
            v.tensor_tensor(lg[:, :, :], ps[:, 0, 0:T * NR].rearrange("p (t n) -> p t n", t=T),
                            biasr[:, :].rearrange("p (a n) -> p a n", a=1).broadcast_to([P, T, NR]),
                            ALU.add).then_inc(lg_read, 1)

            lang, route = lg[:, :, E:NR], lg[:, :, 0:E]

            def over(ap, n):
                return ap.rearrange("p (t a) -> p t a", a=1).broadcast_to([P, T, n])

            dve.wait_ge(lg_read, 1)
            step(v.tensor_reduce(s1[:, 0, :], lang, AX.X, ALU.max))
            v.tensor_tensor(lpp[:, :, 0:L], lang, over(s1[:, 0, :], L), ALU.subtract).then_inc(lang_in, 1)
            dve.wait_ge(lang_exp, 1)
            step(v.tensor_reduce(s1[:, 1, :], le[:, :, :], AX.X, ALU.add))
            step(v.reciprocal(s1[:, 2, :], s1[:, 1, :]))
            step(v.tensor_tensor(lpp[:, :, 0:L], le[:, :, :], over(s1[:, 2, :], L), ALU.mult))
            step(v.tensor_tensor(le[:, :, :], lpp[:, :, 0:L], lpp[:, :, 1:L + 1], ALU.add))
            for q in range(E // L):
                last = v.scalar_tensor_tensor(out=route[:, :, q * L:(q + 1) * L], in0=le[:, :, :], scalar=0.1,
                                              in1=route[:, :, q * L:(q + 1) * L], op0=ALU.mult, op1=ALU.add)
            step(last)

            def pick(k, logits, m):
                step(v.tensor_reduce(s1[:, m, :], logits, AX.X, ALU.max))
                step(v.tensor_tensor(eq[:, :, :], logits, over(s1[:, m, :], E), ALU.is_equal))
                step(v.tensor_tensor(eq[:, :, :], eq[:, :, :],
                                     first[:, :].rearrange("p (a e) -> p a e", a=1).broadcast_to([P, T, E]), ALU.mult))
                step(v.tensor_reduce(s1[:, 3, :], eq[:, :, :], AX.X, ALU.max))
                step(v.tensor_tensor(oh[:, k, :, :], eq[:, :, :], over(s1[:, 3, :], E), ALU.is_equal))

            pick(0, route, 6)
            step(v.scalar_tensor_tensor(out=r2[:, :, :], in0=oh[:, 0, :, :], scalar=-BIG, in1=route,
                                        op0=ALU.mult, op1=ALU.add))
            pick(1, r2[:, :, :], 7)
            step(v.tensor_tensor(M16[:, :, :], oh[:, 0, :, :], oh[:, 1, :, :], ALU.add))
            with nc.allow_low_precision(reason="counts of at most 16"):
                v.tensor_reduce(Mt[:, :], M16[:, :, :].rearrange("p t e -> p e t"), AX.X, ALU.add).then_inc(picked, 1)
            v.tensor_tensor(s1[:, 4, :], s1[:, 7, :], s1[:, 6, :], ALU.subtract).then_inc(gap_in, 1)
            dve.wait_ge(counted, 1)
            step(v.tensor_scalar(tli[:, 0, :], ps[:, 3, 0:E], float(P - 1), None, ALU.add))
            step(v.tensor_scalar(tli[:, 1, :], tli[:, 0, :], 7, None, ALU.logical_shift_right))
            dve.wait_ge(gap_exp, 1)
            beside(v.tensor_scalar(s1[:, 0, :], s1[:, 5, :], 1.0, None, ALU.add))
            step(v.tensor_scalar(tl[:, 0, L:], tli[:, 1, :], -1.0, 0.0, ALU.add, ALU.max))
            beside(v.reciprocal(s1[:, 1, :], s1[:, 0, :]))
            step(v.tensor_tensor(tl[:, 1, L:], tl[:, 0, L:], tl[:, 0, L - 1:L + E - 1], ALU.add))
            beside(v.tensor_tensor(s1[:, 2, :], s1[:, 5, :], s1[:, 1, :], ALU.mult))
            step(v.tensor_tensor(tl[:, 2, L:], tl[:, 1, L:], tl[:, 1, L - 2:L + E - 2], ALU.add))
            beside(v.tensor_tensor(eq[:, :, :], oh[:, 0, :, :], over(s1[:, 1, :], E), ALU.mult))
            step(v.tensor_tensor(tl[:, 3, L:], tl[:, 2, L:], tl[:, 2, L - 4:L + E - 4], ALU.add))
            ends = tl[:, 3, L:]
            beside(v.tensor_tensor(r2[:, :, :], oh[:, 1, :, :], over(s1[:, 2, :], E), ALU.mult))
            step(v.tensor_tensor(base[:, 0, :], ends, tl[:, 0, L:], ALU.subtract))
            v.tensor_tensor(payv[:, :, D:ROW], eq[:, :, :], r2[:, :, :], ALU.add).then_inc(p_ready, 1)
            step(v.tensor_scalar(base[:, 1, :], base[:, 0, :], float(P), float((E - 1) * P), ALU.mult, ALU.add))
            step(v.tensor_tensor(base[:, 2, :], base[:, 1, :], home[:, :], ALU.subtract))
            rank = ps[:, 2, 0:T * E].rearrange("p (t e) -> p t e", e=E)

            def each(ap):
                return ap.rearrange("p (a e) -> p a e", a=1).broadcast_to([P, T, E])

            dve.wait_ge(p_ready, 1)
            dve.wait_ge(ranked, 1)
            step(v.scalar_tensor_tensor(out=eq[:, :, :], in0=rank, scalar=float(P), in1=each(base[:, 2, :]),
                                        op0=ALU.is_ge, op1=ALU.mult))
            step(v.tensor_tensor(r2[:, :, :], rank, eq[:, :, :], ALU.add))
            step(v.tensor_tensor(eq[:, :, :], r2[:, :, :], each(home[:, :]), ALU.add))
            step(v.tensor_tensor(own[:, :, :, :], oh[:, :, :, :], eq[:, :, :].rearrange(
                "p (a t) e -> p a t e", a=1).broadcast_to([P, K, T, E]), ALU.mult))
            with nc.allow_low_precision(reason="slots are whole numbers below 2^13"):
                step(v.tensor_reduce(slot[:, 0, :], own[:, :, :, :].rearrange("p k t e -> p (k t) e"), AX.X, ALU.add))
            v.tensor_scalar(slot[:, 2, :], slot[:, 0, :], P - 1, None, ALU.bitwise_and)
            step(v.tensor_scalar(slot[:, 1, :], slot[:, 0, :], 7, None, ALU.logical_shift_right))

            def every(q, n):
                return slot[:, q:q + 1, :].broadcast_to([P, n, K * T])

            dve.wait_ge(iota_ready, 1)
            v.tensor_tensor(tilehot[:, :, :], iota[:, 0:NT, :], every(1, NT), ALU.is_equal).then_inc(tile_hot, 1)
            v.tensor_tensor(ohv[:, :, :], iota[:, :, :], every(2, P), ALU.is_equal)
            dve.wait_ge(tile_hot, 1)
            v.tensor_tensor(tilehot[:, :, :], tilehot[:, :, :], tok16[:, :].rearrange("p (a c) -> p a c", a=1).broadcast_to(
                [P, NT, K * T]), ALU.mult).then_inc(hot_ready, 1)

            step(v.tensor_tensor(cmp[:, :, :], tiles_i[:, :, :],
                                 tl[0:1, 3:4, L:].broadcast_to([1, NT - E, E]), ALU.is_ge))
            step(v.tensor_reduce(tef[:, :], cmp[:, :, :], AX.X, ALU.add))
            v.tensor_scalar(te[:, E:NT], tef[:, :], float(E - 1), None, ALU.min).then_inc(te_ready, 1)
            dve.wait_ge(b1_max, 1)
            step(v.tensor_scalar(bfield[:, :], bmax[:, :].bitcast(I32), 23, None, ALU.logical_shift_right))
            step(v.tensor_scalar(nfb[:, :], bfield[:, :], -float(FIELD_HB), -float(FIELD_MAX), ALU.add, ALU.max))
            dve.wait_ge(mapped, 1)
            step(v.tensor_scalar(padv[:, :], ps[:, MB, 0:NT], 0.0, padf[:, 0:1], ALU.is_equal, ALU.mult))
            v.scalar_tensor_tensor(out=idx[:, :], in0=ps[:, MB, 0:NT], scalar=-1.0, in1=padv[:, :],
                                   op0=ALU.add, op1=ALU.add).then_inc(idx_ready, 1)
            dve.wait_ge(y_sq, 4)
            v.tensor_reduce(ysm[:, :], ysum[:, :], AX.X, ALU.max).then_inc(ym_ready, 1)
            split_lo(2)
            dve.wait_ge(y_max, 1)
            step(v.tensor_scalar(yt[:, :], ymax[:, :].bitcast(I32), 24, None, ALU.logical_shift_right))
            v.tensor_scalar(yscale[:, :].bitcast(I32), yt[:, :], -ULP, FIELD_SCALE * ULP, ALU.mult,
                            ALU.add).then_inc(ys_ready, 1)
            v.tensor_scalar(yg[:, 0:1], yt[:, :], -float(FIELD_GELU), None, ALU.add)
            step(v.tensor_scalar(yg[:, 1:2], yt[:, :], -1.0, float(FIELD_H), ALU.mult, ALU.add))
            wt2 = wt[:, :].rearrange("p (e w) -> p e w", w=2)

            def table_done(e):
                return max(e - 1, 1)

            def table_gelu(e0, e1):
                dve.wait_ge(w_t, 2 * e1)
                v.tensor_scalar(tab[:, e0:e1, C_GELU].bitcast(I32), wt2[:, e0:e1, 0], yg[:, 0:1], ULP, ALU.add, ALU.mult)
                v.scalar_tensor_tensor(out=fld[:, 0, e0:e1], in0=wt2[:, e0:e1, 0], scalar=yg[:, 1:2],
                                       in1=nfb[:, e0:e1], op0=ALU.subtract, op1=ALU.max).then_inc(field_h, 1)

            def table_h(e0, e1):
                dve.wait_ge(field_h, table_done(e0))
                v.tensor_scalar(tab[:, e0:e1, C_H].bitcast(I32), fld[:, 0, e0:e1], -ULP, None, ALU.mult)
                v.scalar_tensor_tensor(out=fld[:, 1, e0:e1], in0=wt2[:, e0:e1, 1], scalar=float(FIELD_O),
                                       in1=fld[:, 0, e0:e1], op0=ALU.add, op1=ALU.add).then_inc(field_o, 1)

            def table_o(e0, e1):
                dve.wait_ge(field_o, table_done(e0))
                v.tensor_scalar(tab[:, e0:e1, C_O].bitcast(I32), fld[:, 1, e0:e1], 1.0, ULP, ALU.max,
                                ALU.mult).then_inc(tab_ready, 1)

            table_gelu(0, 3)
            table_h(0, 3)
            table_o(0, 3)

            def split_x(j, s):
                r = s % RING
                dve.wait_ge(x_hi, j + 1)
                v.scalar_tensor_tensor(out=xsp[:, r, 1, :, :].rearrange("p k n -> p (k n)"), in0=ps[:, XB, 0:D],
                                       scalar=yscale[:, 0:1], in1=xsp[:, r, 0, :, :].rearrange("p k n -> p (k n)"),
                                       op0=ALU.mult, op1=ALU.subtract).then_inc(x_split, 1)

            def expert_table(j, s, e):
                r = s % RING
                if not (isinstance(j, int) and j < RING):
                    dve.wait_ge(o_ready, j - RING + 1)
                if isinstance(e, int):
                    dve.wait_ge(tab_ready, table_done(e))
                v.tensor_copy(cur[:, r, 0:C_P], tab[:, bass.ds(e, 1), 0:C_P].rearrange("p a c -> p (a c)"))
                v.tensor_copy(cur[:, r, C_P:NCUR], rows[:, s % ROWS, bass.ds(e + D, 1)]).then_inc(cur_ready, 1)

            def parts_of_h(s, gg):
                n = (2 * s + gg) % NH
                return [hsp[:, n, part, :, :].rearrange("p c n -> p (c n)") for part in range(2)]

            def high_h(j, s):
                dve.wait_ge(gelu_done, 2 * j + 2)
                v.tensor_scalar(parts_of_h(s, 1)[0], h32[:, 1, :], cur[:, s % RING, C_H:C_H + 1], None,
                                ALU.mult).then_inc(h_hi_dve, 1)

            def low_h(j, s, gg):
                hi, lo = parts_of_h(s, gg)
                if gg == 0:
                    dve.wait_ge(h_hi_act, j + 1)
                else:
                    dve.wait_ge(h_hi_dve, j + 1)
                v.scalar_tensor_tensor(out=lo, in0=h32[:, gg, :], scalar=cur[:, s % RING, C_H:C_H + 1], in1=hi,
                                       op0=ALU.mult, op1=ALU.subtract).then_inc(h_split, 1)

            def rows_high(j, s, e):
                r = s % RING
                dve.wait_ge(l2_done, j + 1)
                if not (isinstance(j, int) and j < RING):
                    dve.wait_ge(added, 16 * (j - RING + 1))
                v.scalar_tensor_tensor(out=outb[:, r, :], in0=ps[:, OB + r, 0:D], scalar=cur[:, r, C_O:C_O + 1],
                                       in1=b2bc[:, bass.ds(e, 1), :].rearrange("p a d -> p (a d)"),
                                       op0=ALU.mult, op1=ALU.add).then_inc(o_sum, 1)

            def rows_low(j, s):
                r = s % RING
                dve.wait_ge(o_sum, j + 1)
                v.scalar_tensor_tensor(out=outb[:, r, :], in0=ps[:, OB + r, D:2 * D], scalar=cur[:, r, C_O:C_O + 1],
                                       in1=outb[:, r, :], op0=ALU.mult, op1=ALU.add).then_inc(o_read, 1)

            def turn(j, s, first=False, turned=True, split=()):
                e_out = None if first else expert_of(ON_DVE, j - 1)
                e_in = expert_of(ON_DVE, j + 2) if turned else None
                high_h(j, s)
                if isinstance(j, int) and 1 <= j <= E - 3:
                    table_o(j + 2, j + 3)
                if not split:
                    low_h(j, s, 1)
                if turned:
                    split_x(j + 2, s + 2)
                if split:
                    low_h(j, s, 1)
                for n in split[:1]:
                    split_lo(n)
                if not first:
                    if isinstance(j, int) and j == 1:
                        dve.wait_ge(b2_in, 16)
                    rows_high(j - 1, s - 1, e_out)
                    if not split:
                        rows_low(j - 1, s - 1)
                low_h(j + 1, s + 1, 0)
                if split and not first:
                    rows_low(j - 1, s - 1)
                for n in split[1:]:
                    table_gelu(n // 2, n // 2 + 1)
                    split_lo(n)
                    table_h(n // 2, n // 2 + 1)
                if turned:
                    expert_table(j + 2, s + 2, e_in)

            split_lo(3)
            dve.wait_ge(y_written, 16 * 4)
            for j in range(2):
                split_x(j, j)
                expert_table(j, j, j)
            split_lo(4)
            low_h(0, 0, 0)
            split_lo(5)
            dve.wait_ge(te_ready, 1)
            for j in range(PEELED * RING):
                turn(j, j, first=(j == 0),
                     split=range(GAP + 2 * j, min(GAP + 2 * j + 2, 2 * E)))
            with dve.Fori(0, (LAST - PEELED) // BODY) as i:
                for u in range(BODY * RING):
                    turn(RING * PEELED + RING * BODY * i + u, RING * PEELED + u)
            turn(NT - 3, NT - 3)
            turn(NT - 2, NT - 2, turned=False)
            high_h(NT - 1, NT - 1)
            low_h(NT - 1, NT - 1, 1)
            for j in (NT - 2, NT - 1):
                rows_high(j, j, expert_of(ON_DVE, j))
                rows_low(j, j)


_INS = ["x", "cond_1024", "L0_cond_weight", "L0_ffn_router_w", "L0_ffn_router_b", "L0_ffn_lang_w", "L0_ffn_lang_b",
        "L0_ffn_w1", "L0_ffn_b1", "L0_ffn_w2", "L0_ffn_b2"]


def kernel(**inputs):
    import numpy as _np
    import concourse.bacc as _bacc
    from concourse import mybir as _mybir
    from concourse.bass_utils import run_bass_kernel_spmd as _run

    nc = _bacc.Bacc("TRN2", target_bir_lowering=False, num_devices=1)
    arrays, args = {}, []
    for name in _INS:
        a = _np.ascontiguousarray(inputs[name])
        arrays[f"in_{name}"] = a
        args.append(nc.dram_tensor(f"in_{name}", a.shape, _mybir.dt.from_np(a.dtype), kind="ExternalInput").ap())
    args.append(nc.dram_tensor("out_0", (N + P, D), _mybir.dt.float32, kind="ExternalOutput").ap())
    adaln_moe(nc, *args)
    r = _run(nc, [arrays], core_ids=[0])
    return r.results[0]["out_0"][0:N].reshape(NB, SEQ, D)
```
